# Optimizing a Trainium2 kernel written in Bass

```python
import numpy as np
import jax
import jax.numpy as jnp

def _softmax(x, axis=-1):
    return jax.nn.softmax(x, axis=axis)

def _gelu(x):
    return jax.nn.gelu(x, approximate=True)

def _silu(x):
    return jax.nn.silu(x)

def _sigmoid(x):
    return jax.nn.sigmoid(x)

def _layernorm(x, axis=-1, eps=1e-05):
    m = jnp.mean(x, axis=axis, keepdims=True)
    v = jnp.var(x, axis=axis, keepdims=True)
    return (x - m) / jnp.sqrt(v + eps)

def _scatter_add(tgt, idx, src, axis=0):
    return tgt.at[idx].add(src)

def _segment_sum(src, seg, n):
    return jax.ops.segment_sum(src, seg, n)
kernel_name = 'mk_seq_preln_d1_jaxref_r8_e00280'

def setup_inputs(seed: int=0):
    np.random.seed(seed)
    _w = jnp.asarray

    def _L0_attn_setup():
        import jax, jax.numpy as jnp
        import numpy as np
        D_MODEL = 128
        N_HEADS = 16
        D_HEAD = D_MODEL // N_HEADS
        RPE_HIDDEN = 32

        def _rpe_bias(T, w1, b1, w2, b2):
            pos = jnp.arange(T, dtype=jnp.float32)
            rel = pos[:, None] - pos[None, :]
            rel = jnp.sign(rel) * jnp.log1p(jnp.abs(rel))
            h = jax.nn.relu(rel[..., None] * w1[0] + b1)
            bias = h @ w2 + b2
            return jnp.transpose(bias, (2, 0, 1))
        key = jax.random.key(seed)
        ks = jax.random.split(key, 8)
        B, T = (2, 256)
        s = lambda fan_in: 1.0 / np.sqrt(fan_in)
        return {'x': jax.random.normal(ks[0], (B, T, D_MODEL), dtype=jnp.float32), 'w_qkv': jax.random.uniform(ks[1], (D_MODEL, 3 * D_MODEL), jnp.float32, -s(D_MODEL), s(D_MODEL)), 'b_qkv': jnp.zeros((3 * D_MODEL,), jnp.float32), 'w_out': jax.random.uniform(ks[2], (D_MODEL, D_MODEL), jnp.float32, -s(D_MODEL), s(D_MODEL)), 'b_out': jnp.zeros((D_MODEL,), jnp.float32), 'w1_rpe': jax.random.uniform(ks[3], (1, RPE_HIDDEN), jnp.float32, -1.0, 1.0), 'b1_rpe': jax.random.uniform(ks[4], (RPE_HIDDEN,), jnp.float32, -1.0, 1.0), 'w2_rpe': jax.random.uniform(ks[5], (RPE_HIDDEN, N_HEADS), jnp.float32, -s(RPE_HIDDEN), s(RPE_HIDDEN)), 'b2_rpe': jnp.zeros((N_HEADS,), jnp.float32)}
    _L0_attn_in = _L0_attn_setup()

    def _L0_ffn_setup():
        import jax, jax.numpy as jnp
        import numpy as np
        TOP_K = 2
        key = jax.random.key(seed)
        k0, k1, k2, k3, k4 = jax.random.split(key, 5)
        B, S, D, H, E = (4, 256, 128, 256, 8)
        x = jax.random.normal(k0, (B, S, D), dtype=jnp.float32)
        router_w = jax.random.normal(k1, (E, D), dtype=jnp.float32) * D ** (-0.5)
        w_gate = jax.random.normal(k2, (E, D, H), dtype=jnp.float32) * D ** (-0.5)
        w_up = jax.random.normal(k3, (E, D, H), dtype=jnp.float32) * D ** (-0.5)
        w_down = jax.random.normal(k4, (E, H, D), dtype=jnp.float32) * H ** (-0.5)
        return {'x': x, 'router_w': router_w, 'w_gate': w_gate, 'w_up': w_up, 'w_down': w_down}
    _L0_ffn_in = _L0_ffn_setup()
    _d = {'L0_attn_x': _L0_attn_in['x'], 'L0_attn_w_qkv': _L0_attn_in['w_qkv'], 'L0_attn_b_qkv': _L0_attn_in['b_qkv'], 'L0_attn_w_out': _L0_attn_in['w_out'], 'L0_attn_b_out': _L0_attn_in['b_out'], 'L0_attn_w1_rpe': _L0_attn_in['w1_rpe'], 'L0_attn_b1_rpe': _L0_attn_in['b1_rpe'], 'L0_attn_w2_rpe': _L0_attn_in['w2_rpe'], 'L0_attn_b2_rpe': _L0_attn_in['b2_rpe'], 'L0_ffn_router_w': _L0_ffn_in['router_w'], 'L0_ffn_w_gate': _L0_ffn_in['w_gate'], 'L0_ffn_w_up': _L0_ffn_in['w_up'], 'L0_ffn_w_down': _L0_ffn_in['w_down']}
    _x0 = _d['L0_attn_x']
    _d['L0_attn_x'] = jax.random.normal(jax.random.fold_in(jax.random.key(seed), 1), (4, 1024, 128), dtype=_x0.dtype)
    del _x0
    return _d

def reference(L0_attn_x, L0_attn_w_qkv, L0_attn_b_qkv, L0_attn_w_out, L0_attn_b_out, L0_attn_w1_rpe, L0_attn_b1_rpe, L0_attn_w2_rpe, L0_attn_b2_rpe, L0_ffn_router_w, L0_ffn_w_gate, L0_ffn_w_up, L0_ffn_w_down):

    def _L0_attn_ref(x, w_qkv, b_qkv, w_out, b_out, w1_rpe, b1_rpe, w2_rpe, b2_rpe):
        import jax, jax.numpy as jnp
        import numpy as np
        D_MODEL = 128
        N_HEADS = 16
        D_HEAD = D_MODEL // N_HEADS
        RPE_HIDDEN = 32

        def _rpe_bias(T, w1, b1, w2, b2):
            pos = jnp.arange(T, dtype=jnp.float32)
            rel = pos[:, None] - pos[None, :]
            rel = jnp.sign(rel) * jnp.log1p(jnp.abs(rel))
            h = jax.nn.relu(rel[..., None] * w1[0] + b1)
            bias = h @ w2 + b2
            return jnp.transpose(bias, (2, 0, 1))
        B, T, C = x.shape
        qkv = x @ w_qkv + b_qkv
        q, k, v = jnp.split(qkv, 3, axis=-1)

        def heads(t):
            return jnp.transpose(t.reshape(B, T, N_HEADS, D_HEAD), (0, 2, 1, 3))
        q, k, v = (heads(q), heads(k), heads(v))
        scores = jnp.einsum('bhtd,bhsd->bhts', q, k) / np.sqrt(D_HEAD)
        scores = scores + _rpe_bias(T, w1_rpe, b1_rpe, w2_rpe, b2_rpe)[None]
        attn = jax.nn.softmax(scores, axis=-1)
        out = jnp.einsum('bhts,bhsd->bhtd', attn, v)
        out = jnp.transpose(out, (0, 2, 1, 3)).reshape(B, T, C)
        return out @ w_out + b_out

    def _L0_ffn_ref(x, router_w, w_gate, w_up, w_down):
        import jax, jax.numpy as jnp
        import numpy as np
        TOP_K = 2
        B, S, D = x.shape
        E = router_w.shape[0]
        xt = x.reshape(-1, D)
        logits = xt @ router_w.T
        topk_vals, topk_idx = jax.lax.top_k(logits, TOP_K)
        g = jax.nn.sigmoid(topk_vals)
        g = g / (g.sum(axis=-1, keepdims=True) + 1e-10)
        out = jnp.zeros_like(xt)
        for e in range(E):
            ge = jnp.sum(jnp.where(topk_idx == e, g, jnp.zeros_like(g)), axis=-1)
            h = jax.nn.silu(xt @ w_gate[e]) * (xt @ w_up[e])
            out = out + ge[:, None] * (h @ w_down[e])
        return out.reshape(B, S, D)
    x = L0_attn_x
    x = x + _L0_attn_ref(_layernorm(x, axis=-1), L0_attn_w_qkv, L0_attn_b_qkv, L0_attn_w_out, L0_attn_b_out, L0_attn_w1_rpe, L0_attn_b1_rpe, L0_attn_w2_rpe, L0_attn_b2_rpe)
    x = x + _L0_ffn_ref(_layernorm(x, axis=-1), L0_ffn_router_w, L0_ffn_w_gate, L0_ffn_w_up, L0_ffn_w_down)
    return x

_drawn_inputs = setup_inputs


def setup_inputs(seed=0):
    import zlib

    import numpy as np

    out = dict(_drawn_inputs(seed))
    spreads = {'L0_attn_b_qkv': (0.0, 0.1), 'L0_attn_b_out': (0.0, 0.1), 'L0_attn_b2_rpe': (0.0, 0.8)}
    factors = {'L0_attn_b1_rpe': 5.084}
    for name, (base, spread) in spreads.items():
        noise = np.random.default_rng([zlib.crc32(name.encode()), seed]).standard_normal(out[name].shape)
        drawn = base * np.exp(spread * noise) if base else spread * noise
        out[name] = jnp.asarray(drawn.astype(out[name].dtype))
    for name, factor in factors.items():
        out[name] = (out[name] * factor).astype(out[name].dtype)
    return out
```

```python
import concourse.bass as bass
from concourse import mybir
from contextlib import ExitStack


FP32 = mybir.dt.float32
BF16 = mybir.dt.bfloat16
U32 = mybir.dt.uint32
ALU = mybir.AluOpType
ACT = mybir.ActivationFunctionType
AX = mybir.AxisListType

BATCH, SEQ, DM = 4, 1024, 128
HEADS, DH = 16, 8
RPE = 32
EXPERTS, HID = 8, 256
P = 128
TILES = BATCH * SEQ // P
CH = SEQ // P
GROUPS = TILES // 4
PLANES = 3
ROWS = 96
SHIFT_ROWS = 2 * CH
KROWS = ROWS + SHIFT_ROWS
TABW = SEQ + SEQ - P
NREL = 2 * SEQ

UNITS = HEADS * BATCH
STEPS = UNITS * CH
LEAD = 10
LAG = 3
NORM_AT, SHIFT_AT = 4, 7
ADDED = (1, 4, 7)
BODY = 8 * CH
FIRST = 24
TURNS = (STEPS - FIRST - LEAD) // BODY
LOOP_END = FIRST + TURNS * BODY
ITEMS = 2 * CH + 2


def item_at(k, kind):
    late = 1 if k > NORM_AT else 0
    return {"max": 2 * k + late, "exp": 2 * k + 1 + late, "norm": 2 * NORM_AT + 2, "shift": ITEMS - 1}[kind]


PLACES = [None] * ITEMS
for _k in range(CH):
    PLACES[item_at(_k, "max")] = ("max", _k)
    PLACES[item_at(_k, "exp")] = ("exp", _k)
PLACES[item_at(NORM_AT, "norm")] = ("norm", NORM_AT)
PLACES[item_at(SHIFT_AT, "shift")] = ("shift", SHIFT_AT)


def exists(kind, g):
    n = g // CH
    if kind == "max":
        return 0 <= g + LEAD < STEPS
    if kind == "exp":
        return 0 <= g < STEPS
    if kind == "pv":
        return 0 <= g - LAG < STEPS
    if kind == "norm":
        return g % CH == NORM_AT and 1 <= n <= UNITS
    return g % CH == SHIFT_AT and 0 <= n + 1 < UNITS


def wait_apart(engine, semaphore, value, passed):
    engine.wait_ge(semaphore, value)
    engine.sem_inc(passed, 1)


def build(nc, x, w_qkv, b_qkv, w_out, b_out, w1, b1, w2, b2, router_w, w_gate, w_up, w_down, rel_log, out):
    q_planes = nc.dram_tensor("q_planes", [BATCH, HEADS, PLANES * DH, SEQ], BF16).ap()
    k_planes = nc.dram_tensor("k_planes", [BATCH, HEADS, (2 * PLANES - 1) * DH, SEQ], BF16).ap()
    bias_rows = nc.dram_tensor("bias_rows", [2, HEADS, NREL], FP32).ap()

    with ExitStack() as ctx:
        def sb(name, shape, dt=FP32):
            return ctx.enter_context(nc.sbuf_tensor(name, shape, dt))

        xall = sb("xall", [P, TILES, DM])
        vall = sb("vall", [P, TILES, DM])
        oall = sb("oall", [P, TILES, DM])
        wg = sb("wg", [P, EXPERTS, HID])
        wu = sb("wu", [P, EXPERTS, HID])
        wd = sb("wd", [P, EXPERTS, 2, DM])
        wout = sb("wout", [P, DM])
        bout = sb("bout", [P, DM])
        wr = sb("wr", [P, EXPERTS])
        ident = sb("ident", [P, P])
        identb = sb("identb", [P, P], BF16)
        mirror = sb("mirror", [P, P])
        iota8 = sb("iota8", [P, EXPERTS])
        minus_half = sb("minus_half", [P, TILES])
        area = sb("area", [P, 8 * SEQ + 4 * TABW])
        ps = ctx.enter_context(nc.psum_tensor("ps", [P, 8, 512], FP32))

        qst = [sb(f"qst{i}", [P, SEQ], BF16) for i in range(4)]
        kst = [sb(f"kst{i}", [P, SEQ], BF16) for i in range(4)]
        vst = [sb(f"vst{i}", [P, CH, 32]) for i in range(2)]
        shifts = sb("shifts", [P, CH * SHIFT_ROWS], BF16)

        prepare(nc, x, w_qkv, b_qkv, w_out, b_out, w1, b1, w2, b2, router_w, w_gate, w_up, w_down, rel_log,
                q_planes, k_planes, bias_rows, xall, vall, wg, wu, wd, wout, bout, wr, ident, identb, mirror, iota8,
                minus_half, area, ps, qst, kst, vst, shifts)
        attend(nc, q_planes, k_planes, bias_rows, vall, oall, ident, identb, area, ps, qst, kst, vst, shifts)
        finish(nc, out, xall, oall, wg, wu, wd, wout, bout, wr, ident, iota8, minus_half, ps)


def prepare(nc, x, w_qkv, b_qkv, w_out, b_out, w1, b1, w2, b2, router_w, w_gate, w_up, w_down, rel_log,
            q_planes, k_planes, bias_rows, xall, vall, wg, wu, wd, wout, bout, wr, ident, identb, mirror, iota8,
            minus_half, area, ps, qst, kst, vst, shifts):
    with ExitStack() as ctx:
        def sb(name, shape, dt=FP32):
            return ctx.enter_context(nc.sbuf_tensor(name, shape, dt))

        def sem(name):
            return ctx.enter_context(nc.semaphore(name))

        half = PLANES * TILES * P // 2
        qp = area[:, 0:half].bitcast(BF16).rearrange("p (j t) -> p j t", j=PLANES)
        kp = area[:, half:2 * half].bitcast(BF16).rearrange("p (j t) -> p j t", j=PLANES)
        wqkv = sb("wqkv", [P, 3 * DM])
        bq = sb("bq", [P, 1])
        bk = sb("bk", [P, 1])
        bv = sb("bv", [P, DM])
        rel = sb("rel", [RPE, NREL])
        hid = sb("hid", [RPE, NREL])
        w1c = sb("w1c", [RPE, 1])
        b1c = sb("b1c", [RPE, 1])
        w2s = sb("w2s", [RPE, HEADS])
        b2c = sb("b2c", [HEADS, 1])
        bias = sb("bias", [HEADS, NREL])
        ebias = sb("ebias", [HEADS, NREL])
        bmax = sb("bmax", [HEADS, 1])
        stats = sb("stats", [P, TILES, 6])
        mv = sb("mv", [P, TILES, 2])
        rstd = sb("rstd", [P, TILES])
        xn = sb("xn", [P, 4, DM])
        xt = sb("xt", [P, 512])
        xt_rev = sb("xt_rev", [P, 512])
        qf = sb("qf", [P, 512])
        kf = sb("kf", [P, 512])
        kr = sb("kr", [P, 512])
        qr = sb("qr", [P, 512])

        x_loaded = sem("x_loaded")
        small_loaded = sem("small_loaded")
        weights_loaded = sem("weights_loaded")
        const_ready = sem("const_ready")
        v_zeroed = sem("v_zeroed")
        stats_ready = sem("stats_ready")
        aggr_ready = sem("aggr_ready")
        rstd_ready = sem("rstd_ready")
        hidden_ready = sem("hidden_ready")
        bias_ps = sem("bias_ps")
        bias_chain = sem("bias_chain")
        bias_ready = sem("bias_ready")
        ebias_ready = sem("ebias_ready")
        bias_stored = sem("bias_stored")
        xn_ready = sem("xn_ready")
        xt_ps = sem("xt_ps")
        xt_ready = sem("xt_ready")
        qkv_ps = sem("qkv_ps")
        kf_ready = sem("kf_ready")
        v_ready = sem("v_ready")
        split = sem("split")
        ksplit = sem("ksplit")
        planes_stored = sem("planes_stored")
        pool_waits = sem("pool_waits1")

        xt_bank, q_bank, k_bank, v_bank, xt_rev_bank = (ps[:, i, :] for i in range(5))

        with nc.Block() as block:
            @block.sync
            def _(sp):
                sp.dma_start(rel[:, :], rel_log.partition_broadcast(RPE)).then_inc(small_loaded, 16)
                for dst, src in ((w1c, w1.rearrange("a j -> j a")), (b1c, b1.rearrange("(j a) -> j a", a=1)),
                                 (w2s, w2), (b2c, b2.rearrange("(h a) -> h a", a=1)),
                                 (wqkv, w_qkv), (bq, b_qkv[0:DM].rearrange("(c a) -> c a", a=1)),
                                 (bk, b_qkv[DM:2 * DM].rearrange("(c a) -> c a", a=1)),
                                 (bv, b_qkv[2 * DM:3 * DM].partition_broadcast(P))):
                    sp.dma_start(dst[:, :], src).then_inc(small_loaded, 16)
                for dst, src in ((wout[:, :], w_out), (bout[:, :], b_out.partition_broadcast(P)),
                                 (wr[:, :], router_w), (wg[:, :, :], w_gate.rearrange("e d h -> d e h")),
                                 (wu[:, :, :], w_up.rearrange("e d h -> d e h")),
                                 (wd[:, :, :, :], w_down.rearrange("e (c h) d -> h e c d", c=2))):
                    sp.dma_start(dst, src).then_inc(weights_loaded, 16)
                sp.wait_ge(bias_ready, 1)
                sp.dma_start(bias_rows[0, :, :], bias[:, :]).then_inc(bias_stored, 16)
                sp.wait_ge(ebias_ready, 1)
                sp.dma_start(bias_rows[1, :, :], ebias[:, :]).then_inc(bias_stored, 16)
                with sp.Fori(0, BATCH) as b:
                    sp.wait_ge(split, b * 10 + 10)
                    for j in range(PLANES):
                        sp.dma_start(q_planes[b, :, j * DH:(j + 1) * DH, :], qp[:, j, bass.ds(b * SEQ, SEQ)])\
                          .then_inc(planes_stored, 16)
                    sp.wait_ge(ksplit, b * 8 + 8)
                    for j in range(2 * PLANES - 1):
                        sp.dma_start(k_planes[b, :, j * DH:(j + 1) * DH, :],
                                     kp[:, j % PLANES, bass.ds(b * SEQ, SEQ)]).then_inc(planes_stored, 16)
                sp.wait_ge(bias_stored, 32)
                sp.wait_ge(planes_stored, BATCH * (3 * PLANES - 1) * 16)
                sp.wait_ge(weights_loaded, 6 * 16)

            @block.gpsimd
            def _(pool):
                pool.memset(ident[:, :], 0.0).then_inc(const_ready, 1)
                pool.memset(identb[:, :], 0.0).then_inc(const_ready, 1)
                pool.memset(minus_half[:, :], -0.5).then_inc(const_ready, 1)
                pool.iota(iota8[:, :], pattern=[[1, EXPERTS]], base=0, channel_multiplier=0,
                          allow_small_or_imprecise_dtypes=True).then_inc(const_ready, 1)
                pool.memset(mirror[:, :], 0.0).then_inc(const_ready, 1)
                pool.wait_ge(const_ready, 5)
                for m in (ident, identb):
                    pool.affine_select(out=m[:, :], in_=m[:, :], compare_op=ALU.not_equal, fill=1.0, base=0,
                                       pattern=[[-1, P]], channel_multiplier=1).then_inc(const_ready, 1)
                pool.affine_select(out=mirror[:, :], in_=mirror[:, :], compare_op=ALU.not_equal, fill=1.0,
                                   base=1 - P, pattern=[[1, P]], channel_multiplier=1).then_inc(const_ready, 1)
                pool.wait_ge(aggr_ready, 1)
                pool.tensor_scalar(rstd[:, :], mv[:, :, 1], 1e-5, None, ALU.add).then_inc(rstd_ready, 1)
                pool.wait_ge(rstd_ready, 1)
                pool.tensor_tensor(rstd[:, :], rstd[:, :], minus_half[:, :], ALU.pow).then_inc(rstd_ready, 1)

                def split_k(j, side):
                    here = bass.ds((j + 1 - 2 * side) * 512, 512)
                    pool.wait_ge(kf_ready, j + 1)
                    pool.tensor_copy(kp[:, 0, here], kf[:, :]).then_inc(ksplit, 1)
                    wait_apart(pool, ksplit, j * 4 + 1, pool_waits)
                    pool.tensor_tensor(kr[:, :], kf[:, :], kp[:, 0, here], ALU.subtract).then_inc(ksplit, 1)
                    pool.wait_ge(ksplit, j * 4 + 2)
                    pool.tensor_copy(kp[:, 1, here], kr[:, :]).then_inc(ksplit, 1)
                    wait_apart(pool, ksplit, j * 4 + 3, pool_waits)
                    pool.tensor_tensor(kp[:, 2, here], kr[:, :], kp[:, 1, here], ALU.subtract).then_inc(ksplit, 1)

                with pool.Fori(0, BATCH) as b:
                    for side in range(2):
                        split_k(b * 2 + side, side)

            @block.scalar
            def _(act):
                for b in range(BATCH):
                    act.dma_start(xall[:, b * CH:(b + 1) * CH, :], x[b].rearrange("(c p) d -> p c d", p=P))\
                       .then_inc(x_loaded, 16)
                act.wait_ge(small_loaded, 9 * 16)
                nc.scalar.activation(hid[:, :], rel[:, :], ACT.Relu, bias=b1c[:, :], scale=w1c[:, :])\
                  .then_inc(hidden_ready, 1)
                act.wait_ge(bias_ready, 1)
                nc.scalar.activation(ebias[:, :], bias[:, :], ACT.Exp).then_inc(ebias_ready, 1)
                with act.Fori(0, GROUPS) as j:
                    act.wait_ge(xt_ps, j + 1)
                    nc.scalar.copy(xt[:, :], xt_bank)
                    nc.scalar.copy(xt_rev[:, :], xt_rev_bank).then_inc(xt_ready, 1)

            @block.vector
            def _(dve):
                nc.vector.memset(shifts[:, :], 0.0)
                for i in range(4):
                    nc.vector.memset(qst[i][64:ROWS, :], 0.0)
                    nc.vector.memset(kst[i][64:ROWS, :], 0.0)
                    nc.vector.memset(kst[i][ROWS:KROWS, :], 1.0)
                nc.vector.memset(vst[0][:, :, :], 0.0)
                nc.vector.memset(vst[1][:, :, :], 0.0).then_inc(v_zeroed, 1)
                dve.wait_ge(v_zeroed, 1)
                for i in range(2):
                    nc.vector.memset(vst[i][:, :, DH:DH + 1], 1.0)
                dve.wait_ge(bias_ps, 1)
                nc.vector.tensor_scalar(bias[:, :], ps[0:HEADS, 4:8, :].rearrange("h a b -> h (a b)"), b2c[:, :], None,
                                        ALU.add).then_inc(bias_chain, 1)
                dve.wait_ge(bias_chain, 1)
                nc.vector.reduce_max(bmax[:, :], bias[:, :], AX.X).then_inc(bias_chain, 1)
                dve.wait_ge(bias_chain, 2)
                nc.vector.tensor_scalar(bias[:, :], bias[:, :], bmax[:, :], None, ALU.subtract).then_inc(bias_ready, 1)
                dve.wait_ge(x_loaded, BATCH * 16)
                with dve.Fori(0, GROUPS) as j:
                    for q in range(4):
                        nc.vector.bn_stats(stats[:, bass.ds(j * 4 + q, 1), :].rearrange("p a s -> p (a s)"),
                                           xall[:, bass.ds(j * 4 + q, 1), :].rearrange("p a s -> p (a s)"))\
                          .then_inc(stats_ready, 1)
                dve.wait_ge(stats_ready, TILES)
                for tile in range(TILES):
                    last = nc.vector.bn_aggr(mv[:, tile, :], stats[:, tile, :])
                last.then_inc(aggr_ready, 1)
                dve.wait_ge(aggr_ready, 1)
                dve.wait_ge(rstd_ready, 2)

                def normalise(j):
                    for q in range(4):
                        tile = bass.ds(j * 4 + q, 1)
                        last = nc.vector.tensor_scalar(
                            xn[:, q, :], xall[:, tile, :].rearrange("p a s -> p (a s)"),
                            mv[:, tile, 0], rstd[:, tile], ALU.subtract, ALU.mult)
                    last.then_inc(xn_ready, 1)

                def split_q(j, side):
                    here = bass.ds(j * 512, 512)
                    dve.wait_ge(qkv_ps, j + 1)
                    nc.vector.tensor_scalar(qf[:, :], q_bank, bq[:, :], float(DH) ** -0.5, ALU.add, ALU.mult)\
                      .then_inc(split, 1)
                    dve.wait_ge(ksplit, j * 4)
                    nc.vector.tensor_scalar(kf[:, :], k_bank, bk[:, :], None, ALU.add).then_inc(kf_ready, 1)
                    nc.vector.tensor_tensor(vall[:, bass.ds((j + 1 - 2 * side) * 4, 4), :], v_bank.rearrange("p (q c) -> p q c", q=4),
                                            bv[:, :].unsqueeze(1).to_broadcast([P, 4, DM]), ALU.add)\
                      .then_inc(v_ready, 1)
                    dve.wait_ge(split, j * 5 + 1)
                    nc.vector.tensor_copy(qp[:, 0, here], qf[:, :]).then_inc(split, 1)
                    dve.wait_ge(split, j * 5 + 2)
                    nc.vector.tensor_tensor(qr[:, :], qf[:, :], qp[:, 0, here], ALU.subtract).then_inc(split, 1)
                    dve.wait_ge(split, j * 5 + 3)
                    nc.vector.tensor_copy(qp[:, 1, here], qr[:, :]).then_inc(split, 1)
                    dve.wait_ge(split, j * 5 + 4)
                    nc.vector.tensor_tensor(qp[:, 2, here], qr[:, :], qp[:, 1, here], ALU.subtract)\
                      .then_inc(split, 1)

                normalise(0)
                with dve.Fori(0, BATCH - 1) as b:
                    for side in range(2):
                        dve.wait_ge(xt_ps, b * 2 + side + 1)
                        normalise(b * 2 + (side + 1))
                        split_q(b * 2 + side, side)
                dve.wait_ge(xt_ps, GROUPS - 1)
                normalise(GROUPS - 1)
                split_q(GROUPS - 2, 0)
                split_q(GROUPS - 1, 1)

            @block.tensor
            def _(pe):
                pe.wait_ge(hidden_ready, 1)
                for i in range(4):
                    last = nc.tensor.matmul(ps[0:HEADS, 4 + i, :], w2s[:, :], hid[:, i * 512:(i + 1) * 512],
                                            start=True, stop=True)
                last.then_inc(bias_ps, 1)
                pe.wait_ge(bias_chain, 1)
                pe.wait_ge(const_ready, 8)
                pe.wait_ge(small_loaded, 9 * 16)

                def project(j, first):
                    pe.wait_ge(xn_ready, j + 1)
                    if not first:
                        pe.wait_ge(xt_ready, j)
                    for q in range(4):
                        last = nc.tensor.transpose(xt_bank[:, q * P:(q + 1) * P], xn[:, q, :], ident[:, :])
                        last = nc.tensor.transpose(xt_rev_bank[:, (3 - q) * P:(4 - q) * P], xn[:, q, :],
                                                   mirror[:, :])
                    last.then_inc(xt_ps, 1)
                    pe.wait_ge(xt_ready, j + 1)
                    if not first:
                        pe.wait_ge(v_ready, j)
                    nc.tensor.matmul(q_bank, wqkv[:, 0:DM], xt[:, :], start=True, stop=True)
                    nc.tensor.matmul(k_bank, wqkv[:, DM:2 * DM], xt_rev[:, :], start=True, stop=True)
                    for q in range(4):
                        last = nc.tensor.matmul(v_bank[:, q * P:(q + 1) * P], xt_rev[:, q * P:(q + 1) * P],
                                                wqkv[:, 2 * DM:3 * DM], start=True, stop=True)
                    last.then_inc(qkv_ps, 1)

                project(0, True)
                with pe.Fori(1, GROUPS) as j:
                    project(j, False)


def attend(nc, q_planes, k_planes, bias_rows, vall, oall, ident, identb, area, ps, qst, kst, vst, shifts):
    with ExitStack() as ctx:
        def sb(name, shape, dt=FP32):
            return ctx.enter_context(nc.sbuf_tensor(name, shape, dt))

        def sem(name):
            return ctx.enter_context(nc.semaphore(name))

        prob = [area[:, k * SEQ:(k + 1) * SEQ] for k in range(CH)]
        tab0 = CH * SEQ
        bias_tab = [area[:, tab0 + i * TABW:tab0 + (i + 1) * TABW] for i in range(2)]
        mul_tab = [area[:, tab0 + (2 + i) * TABW:tab0 + (3 + i) * TABW] for i in range(2)]
        row_max = [sb(f"row_max{i}", [P, CH]) for i in range(2)]
        ot_sb = [sb(f"ot_sb{i}", [P, 256]) for i in range(2)]
        rden = sb("rden", [P, 2, 4])

        slot = [ps[:, 2 * i:2 * i + 2, :].rearrange("p a b -> p (a b)") for i in range(3)]
        ot_ps = [ps[:, 6 + i, 0:256] for i in range(2)]

        qk_loaded = [sem(f"qk_loaded{i}") for i in range(4)]
        bias_tab_loaded = [sem(f"bias_tab_loaded{i}") for i in range(2)]
        mul_tab_loaded = [sem(f"mul_tab_loaded{i}") for i in range(2)]
        max_scores = sem("max_scores")
        exp_scores = sem("exp_scores")
        shift_ps = sem("shift_ps")
        norm_ps = sem("norm_ps")
        pv_done = sem("pv_done")
        max_done = sem("max_done")
        shifts_high = sem("shifts_high")
        shifts_ready = sem("shifts_ready")
        bias_added = sem("bias_added")
        recip_done = sem("recip_done")
        dve_waits = sem("dve_waits2")
        norm_done = sem("norm_done")
        shift_copied = sem("shift_copied")
        v_staged = sem("v_staged")
        exp_done = sem("exp_done")
        ot_copied = sem("ot_copied")
        bias_multiplied = sem("bias_multiplied")

        def slot_of(kind, k):
            return slot[item_at(k, kind) % 3]

        def count_steps(r, i, more=0):
            return i * BODY + (r + more) if not isinstance(i, int) else i * BODY + r + more

        def count_units(r, i, more=0, per=1):
            return i * (BODY // CH * per) + (r // CH + more) * per

        def run_steps(engine, step):
            for g in range(-LEAD, FIRST):
                step(g, 0, g)
            with engine.Fori(0, TURNS) as i:
                for r in range(FIRST, FIRST + BODY):
                    step(r, i, r)
            for g in range(LOOP_END, STEPS + CH):
                step(g, 0, g)

        added_before = [sum(1 for c in ADDED if c < k) for k in range(CH + 1)]
        multiplied_before = [k - added_before[k] for k in range(CH + 1)]

        with nc.Block() as block:
            @block.sync
            def _(sp):
                def load_tabs(h, turn):
                    for row, tab, loaded in ((0, bias_tab, bias_tab_loaded), (1, mul_tab, mul_tab_loaded)):
                        at = bias_rows[row, h, 0:TABW]
                        sp.dma_start(tab[turn], bass.AP(at.tensor, at.offset, [[1, P], [1, TABW]]))\
                          .then_inc(loaded[turn], 16)

                def load_unit(u, i):
                    head, b, buf = i * 2 + u // BATCH, u % BATCH, u % 4
                    if u >= 4:
                        sp.wait_ge(exp_scores, i * BODY + (u - 3) * CH)
                    for n in range(PLANES):
                        rows = slice(n * PLANES * DH, (n + 1) * PLANES * DH)
                        sp.dma_start(qst[buf][rows, :], q_planes[b, head, :, :]).then_inc(qk_loaded[buf], 16)
                        sp.dma_start(kst[buf][rows, :], k_planes[b, head, n * DH:(n + PLANES) * DH, :])\
                          .then_inc(qk_loaded[buf], 16)

                def unit(u, i):
                    h, turn = u // BATCH, u // BATCH % 2
                    if u % BATCH == 0 and u >= 8:
                        sp.wait_ge(pv_done, i * BODY + (h - 1) * BATCH * CH)
                        load_tabs(i * 2 + h, turn)
                    load_unit(u, i)

                load_tabs(0, 0)
                for u in range(0, 4):
                    load_unit(u, 0)
                load_tabs(1, 1)
                for u in range(4, 8):
                    unit(u, 0)
                with sp.Fori(0, UNITS // 8 - 1) as i:
                    for u in range(8, 16):
                        unit(u, i)

            @block.gpsimd
            def _(pool):
                def step(r, i, g):
                    k, turn = r % CH, r // (BATCH * CH) % 2
                    if not exists("exp", g) or k in ADDED:
                        return
                    if r % (BATCH * CH) == 0:
                        pool.wait_ge(mul_tab_loaded[turn], i * 16 + (r // (2 * BATCH * CH) + 1) * 16)
                    pool.wait_ge(exp_done, count_steps(r, i, 1))
                    pool.tensor_tensor(prob[k], prob[k], mul_tab[turn][:, k * P:k * P + SEQ],
                                       ALU.mult).then_inc(bias_multiplied, 1)

                run_steps(pool, step)

            @block.scalar
            def _(act):
                def step(r, i, g):
                    k, u = r % CH, r // CH
                    if exists("exp", g) and k == 0:
                        if u >= 2:
                            act.wait_ge(pv_done, count_units(r, i, -1, CH))
                        b, h8 = u % BATCH, i * (2 * DH) + u // BATCH * DH
                        nc.scalar.copy(vst[u % 2][:, :, 0:DH], vall[:, b * CH:(b + 1) * CH, bass.ds(h8, DH)])\
                          .then_inc(v_staged, 1)
                        act.wait_ge(shift_ps, count_units(r, i, 1))
                        nc.scalar.copy(qst[u % 4][ROWS:KROWS, :], slot_of("shift", SHIFT_AT)[ROWS:KROWS, :])\
                          .then_inc(shift_copied, 1)
                    if exists("exp", g):
                        if k in ADDED:
                            act.wait_ge(bias_added, count_units(r, i, 0, len(ADDED)) + (added_before[k] + 1))
                        else:
                            act.wait_ge(exp_scores, count_steps(r, i, 1))
                        if r >= CH:
                            act.wait_ge(pv_done, count_steps(r, i, 1 - CH))
                        nc.scalar.activation(prob[k], slot_of("exp", k), ACT.Exp).then_inc(exp_done, 1)
                    if k == LAG and u >= 1 and exists("norm", g - k + NORM_AT):
                        act.wait_ge(pv_done, count_units(r, i, 0, CH))
                        if u >= 3:
                            act.wait_ge(norm_ps, count_units(r, i, -2))
                        nc.scalar.copy(ot_sb[(u - 1) % 2][:, :], ot_ps[(u - 1) % 2]).then_inc(ot_copied, 1)

                run_steps(act, step)

            @block.vector
            def _(dve):
                def step(r, i, g):
                    k, u = r % CH, r // CH
                    if exists("max", g):
                        a = r + LEAD
                        ka, ua, turn = a % CH, a // CH, a // (BATCH * CH) % 2
                        if a % (BATCH * CH) == 0:
                            dve.wait_ge(bias_tab_loaded[turn], i * 16 + (a // (2 * BATCH * CH) + 1) * 16)
                        if ka == 0 and ua >= 2:
                            dve.wait_ge(shifts_ready, count_units(a, i, -1))
                        wait_apart(dve, max_scores, count_steps(a, i, 1), dve_waits)
                        nc.vector.tensor_tensor_reduce(
                            out=slot_of("max", k), in0=slot_of("max", k),
                            in1=bias_tab[turn][:, ka * P:ka * P + SEQ], scale=1.0,
                            scalar=-3.0e38, op0=ALU.add, op1=ALU.max,
                            accum_out=row_max[ua % 2][:, ka:ka + 1]).then_inc(max_done, 1)
                    if exists("exp", g) and k in ADDED:
                        turn = r // (BATCH * CH) % 2
                        dve.wait_ge(exp_scores, count_steps(r, i, 1))
                        s = slot_of("exp", k)
                        nc.vector.tensor_tensor(s, s, bias_tab[turn][:, k * P:k * P + SEQ], ALU.add)\
                          .then_inc(bias_added, 1)
                    if exists("max", g) and ka == CH - 1:
                        dve.wait_ge(max_done, count_steps(a, i, 1))
                        if ua >= 1:
                            dve.wait_ge(shift_ps, count_units(a, i))
                        nc.vector.tensor_scalar(shifts[:, 0:CH * SHIFT_ROWS:SHIFT_ROWS + 1], row_max[ua % 2][:, :],
                                                -1.0, None, ALU.mult).then_inc(shifts_high, 1)
                        dve.wait_ge(shifts_high, count_units(a, i, 1))
                        nc.vector.scalar_tensor_tensor(shifts[:, CH:CH * SHIFT_ROWS:SHIFT_ROWS + 1],
                                                       row_max[ua % 2][:, :], -1.0,
                                                       shifts[:, 0:CH * SHIFT_ROWS:SHIFT_ROWS + 1],
                                                       ALU.mult, ALU.subtract).then_inc(shifts_ready, 1)
                    if exists("norm", g):
                        dve.wait_ge(norm_ps, count_units(r, i))
                        o = slot_of("norm", k)[:, 0:256].rearrange("p (i j c) -> p i j c", i=2, j=4)
                        nc.vector.reciprocal(rden[:, :, :], o[:, :, :, DH]).then_inc(recip_done, 1)
                        dve.wait_ge(recip_done, count_units(r, i))
                        b, h8 = (u - 1) % BATCH, i * (2 * DH) + (u - 1) // BATCH * DH
                        dst = oall[:, b * CH:(b + 1) * CH, bass.ds(h8, DH)].rearrange("p (j i) d -> p i j d", j=4)
                        nc.vector.tensor_tensor(dst, o[:, :, :, 0:DH],
                                                rden[:, :, :].unsqueeze(3).to_broadcast([P, 2, 4, DH]), ALU.mult)\
                          .then_inc(norm_done, 1)

                run_steps(dve, step)
                dve.wait_ge(norm_done, UNITS)

            @block.tensor
            def _(pe):
                def await_slot(kind, r, i, g):
                    at, gu, ru = item_at(r % CH, kind), g // CH, r // CH
                    for back in range(3, 31, 3):
                        du, place = divmod(at - back, ITEMS)
                        was, k = PLACES[place]
                        if (gu + du) * CH + k < -LEAD:
                            return
                        if exists(was, (gu + du) * CH + k):
                            break
                    rr = (ru + du) * CH + k
                    if was == "max":
                        pe.wait_ge(max_done, count_steps(rr, i, LEAD + 1))
                    elif was == "exp":
                        pe.wait_ge(exp_done, count_steps(rr, i, 1))
                    elif was == "norm":
                        pe.wait_ge(norm_done, count_units(rr, i))
                    else:
                        pe.wait_ge(shift_copied, count_units(rr, i, 2))

                def step(r, i, g):
                    k, u = r % CH, r // CH
                    if exists("max", g):
                        a = r + LEAD
                        ka, ua = a % CH, a // CH
                        if ka == 0:
                            pe.wait_ge(qk_loaded[ua % 4], i * (2 * 96) + (ua // 4 + 1) * 96)
                        await_slot("max", r, i, g)
                        q, kk, dst = qst[ua % 4], kst[ua % 4], slot_of("max", k)
                        for c in range(2):
                            last = nc.tensor.matmul(dst[:, c * 512:(c + 1) * 512], q[0:ROWS, ka * P:(ka + 1) * P],
                                                    kk[0:ROWS, c * 512:(c + 1) * 512], start=True, stop=True)
                        last.then_inc(max_scores, 1)
                    if exists("exp", g):
                        if k == 0:
                            pe.wait_ge(shift_copied, count_units(r, i, 1))
                        await_slot("exp", r, i, g)
                        q, kk, dst = qst[u % 4], kst[u % 4], slot_of("exp", k)
                        for c in range(2):
                            last = nc.tensor.matmul(dst[:, c * 512:(c + 1) * 512], kk[0:KROWS, k * P:(k + 1) * P],
                                                    q[0:KROWS, c * 512:(c + 1) * 512], start=True, stop=True)
                        last.then_inc(exp_scores, 1)
                    if exists("pv", g):
                        c = r - LAG
                        kc, uc = c % CH, c // CH
                        if kc == 0:
                            pe.wait_ge(v_staged, count_units(c, i, 1))
                            if uc >= 2:
                                pe.wait_ge(ot_copied, count_units(c, i, -1))
                        if kc in ADDED:
                            pe.wait_ge(exp_done, count_steps(c, i, 1))
                        else:
                            pe.wait_ge(bias_multiplied, count_units(c, i, 0, CH - len(ADDED))
                                       + (multiplied_before[kc] + 1))
                        for j in range(4):
                            last = nc.tensor.matmul(ot_ps[uc % 2][32 * j:32 * j + 32, :], vst[uc % 2][:, kc, :],
                                                    prob[kc][:, 256 * j:256 * j + 256],
                                                    start=(kc == 0), stop=(kc == CH - 1))
                        last.then_inc(pv_done, 1)
                    if exists("norm", g):
                        await_slot("norm", r, i, g)
                        pe.wait_ge(ot_copied, count_units(r, i))
                        for c in range(2):
                            last = nc.tensor.transpose(slot_of("norm", k)[:, c * P:(c + 1) * P],
                                                       ot_sb[(u - 1) % 2][:, c * P:(c + 1) * P], ident[:, :])
                        last.then_inc(norm_ps, 1)
                    if exists("shift", g):
                        await_slot("shift", r, i, g)
                        pe.wait_ge(shifts_ready, count_units(r, i, 2))
                        for c in range(CH):
                            last = nc.tensor.matmul(slot_of("shift", k)[ROWS:KROWS, c * P:(c + 1) * P],
                                                    shifts[:, c * SHIFT_ROWS:(c + 1) * SHIFT_ROWS], identb[:, :],
                                                    start=True, stop=True)
                        last.then_inc(shift_ps, 1)

                run_steps(pe, step)


def finish(nc, out, xall, oall, wg, wu, wd, wout, bout, wr, ident, iota8, minus_half, ps):
    out_t = out.rearrange("b (c p) d -> p (b c) d", p=P)
    with ExitStack() as ctx:
        def sb(name, shape, dt=FP32):
            return ctx.enter_context(nc.sbuf_tensor(name, shape, dt))

        def sem(name):
            return ctx.enter_context(nc.semaphore(name))

        o_in = sb("o_in", [P, 4, DM])
        o_t = sb("o_t", [P, 512])
        y = [sb(f"y{i}", [P, 4, DM]) for i in range(2)]
        stats = sb("stats2", [P, 4, 6])
        mv = sb("mv2", [P, 4, 2])
        rstd = sb("rstd2", [P, 4])
        xn = sb("xn2", [P, 4, DM])
        xt = [sb(f"xt{i}", [P, 512]) for i in range(2)]
        logits = sb("logits", [P, 4, EXPERTS])
        top = sb("top", [P, 4, EXPERTS])
        top_at = sb("top_at", [P, 4, EXPERTS], U32)
        at = sb("at", [P, 4, 2])
        sig = sb("sig", [P, 4, 2])
        total = sb("total", [P, 4])
        gates = sb("gates", [P, 4, 2])
        gate1 = sb("gate1", [P, 4, EXPERTS])
        gate2 = sb("gate2", [P, 4, EXPERTS])
        ge = [sb(f"ge{i}", [P, 4, EXPERTS]) for i in range(2)]
        sg = [sb(f"sg{i}", [P, 512]) for i in range(2)]
        silu = [sb(f"silu{i}", [P, 512]) for i in range(2)]
        hidden = [sb(f"hidden{i}", [P, 2, 512]) for i in range(2)]

        gu_ps = [(ps[:, 2 * c, :], ps[:, 2 * c + 1, :]) for c in range(2)]
        down_ps = [ps[:, 4 + i, :] for i in range(2)]
        side_ps = [ps[:, 6 + i, :] for i in range(2)]

        o_staged = sem("o_staged")
        o_t_ps = sem("o_t_ps")
        o_t_ready = sem("o_t_ready")
        proj_ps = sem("proj_ps")
        var_ready = sem("var_ready")
        rstd_ready = sem("rstd_ready2")
        xn_ready = sem("xn_ready2")
        xt_ps = sem("xt_ps2")
        xt_ready = sem("xt_ready2")
        logits_ps = sem("logits_ps")
        top_ready = sem("top_ready")
        sig_ready = sem("sig_ready")
        chain = sem("chain")
        pow_chain = sem("pow_chain")
        dve_waits = sem("dve_waits3")
        pool_waits = sem("pool_waits3")
        gu_ready = sem("gu_ready")
        sg_ready = sem("sg_ready")
        silu_ready = sem("silu_ready")
        hidden_ready = sem("hidden_ready2")
        down_ready = sem("down_ready")
        added = sem("added")
        stored = [sem(f"stored{i}") for i in range(2)]
        CHAIN = 14

        FRONT_AT = (0, 1, 3, 5)

        def run_groups(engine, front, expert):
            for n in range(4):
                front(n, 0, 0)
            with engine.Fori(0, GROUPS // 2 - 1) as i:
                for t in range(2):
                    for e in range(EXPERTS):
                        expert(e, i * 2 + t, t, False)
                        if e in FRONT_AT:
                            front(FRONT_AT.index(e), i * 2 + (t + 1), 1 - t)
            for t in range(2):
                for e in range(EXPERTS):
                    expert(e, GROUPS - 2 + t, t, True)
                    if e in FRONT_AT and t == 0:
                        front(FRONT_AT.index(e), GROUPS - 1, 1)

        def known(j, least):
            return not isinstance(j, int) or j >= least

        with nc.Block() as block:
            @block.sync
            def _(sp):
                def store(j, t):
                    sp.wait_ge(added, j * EXPERTS + EXPERTS)
                    sp.dma_start(out_t[:, bass.ds(j * 4, 4), :], y[t][:, :, :]).then_inc(stored[t], 16)

                with sp.Fori(0, GROUPS // 2) as i:
                    for t in range(2):
                        store(i * 2 + t, t)
                for t in range(2):
                    sp.wait_ge(stored[t], GROUPS // 2 * 16)

            @block.gpsimd
            def _(pool):
                with pool.Fori(0, GROUPS) as j:
                    wait_apart(pool, var_ready, j + 1, pool_waits)
                    pool.tensor_scalar(rstd[:, :], mv[:, :, 1], 1e-5, None, ALU.add).then_inc(pow_chain, 1)
                    pool.wait_ge(pow_chain, j + 1)
                    pool.tensor_tensor(rstd[:, :], rstd[:, :], minus_half[:, 0:4], ALU.pow).then_inc(rstd_ready, 1)

            @block.scalar
            def _(act):
                def front(n, j, t):
                    if n == 0:
                        if known(j, 1):
                            act.wait_ge(o_t_ps, j)
                        nc.scalar.copy(o_in[:, :, :], oall[:, bass.ds(j * 4, 4), :]).then_inc(o_staged, 1)
                        act.wait_ge(o_t_ps, j + 1)
                        if known(j, 1):
                            act.wait_ge(proj_ps, j)
                        nc.scalar.copy(o_t[:, :], side_ps[0]).then_inc(o_t_ready, 1)
                    if n == 2:
                        act.wait_ge(xt_ps, j + 1)
                        nc.scalar.copy(xt[t][:, :], side_ps[0]).then_inc(xt_ready, 1)
                    if n == 3:
                        act.wait_ge(top_ready, j + 1)
                        nc.scalar.activation(sig[:, :, :], top[:, :, 0:2], ACT.Sigmoid).then_inc(sig_ready, 1)

                def expert(e, j, t, is_last):
                    for c in range(2):
                        m = 2 * e + c
                        act.wait_ge(gu_ready, j * 16 + m + 1)
                        if known(j, 1) or e:
                            act.wait_ge(silu_ready, j * 16 + max(m - 1, 0))
                        nc.scalar.activation(sg[c][:, :], gu_ps[c][0], ACT.Sigmoid).then_inc(sg_ready, 1)

                run_groups(act, front, expert)

            @block.vector
            def _(dve):
                def front(n, j, t):
                    base = j * CHAIN
                    if n == 1:
                        dve.wait_ge(proj_ps, j + 1)
                        if known(j, 2):
                            if isinstance(j, int):
                                dve.wait_ge(stored[t], j // 2 * 16)
                            else:
                                dve.wait_ge(stored[t], stored_before(j, t))
                        nc.vector.tensor_tensor(y[t][:, :, :], side_ps[1].rearrange("p (q c) -> p q c", q=4),
                                                xall[:, bass.ds(j * 4, 4), :], ALU.add).then_inc(chain, 1)
                        dve.wait_ge(chain, base + 1)
                        nc.vector.tensor_tensor(y[t][:, :, :], y[t][:, :, :],
                                                bout[:, :].unsqueeze(1).to_broadcast([P, 4, DM]), ALU.add)\
                          .then_inc(chain, 1)
                        dve.wait_ge(chain, base + 2)
                        for q in range(4):
                            last = nc.vector.bn_stats(stats[:, q, :], y[t][:, q, :])
                        last.then_inc(chain, 1)
                        wait_apart(dve, chain, base + 3, dve_waits)
                        for q in range(4):
                            last = nc.vector.bn_aggr(mv[:, q, :], stats[:, q, :])
                        last.then_inc(var_ready, 1)
                    if n == 2:
                        dve.wait_ge(var_ready, j + 1)
                        dve.wait_ge(rstd_ready, j + 1)
                        for q in range(4):
                            last = nc.vector.tensor_scalar(xn[:, q, :], y[t][:, q, :], mv[:, q, 0:1],
                                                           rstd[:, q:q + 1], ALU.subtract, ALU.mult)
                        last.then_inc(xn_ready, 1)
                    if n == 3:
                        dve.wait_ge(logits_ps, j + 1)
                        nc.vector.tensor_copy(logits[:, :, :], side_ps[1][:, 0:4 * EXPERTS]
                                              .rearrange("p (q e) -> p q e", q=4)).then_inc(chain, 1)
                        wait_apart(dve, chain, base + 4, dve_waits)
                        for q in range(4):
                            last = nc.vector.max(top[:, q, :], logits[:, q, :])
                        last.then_inc(top_ready, 1)
                        wait_apart(dve, top_ready, j + 1, dve_waits)
                        for q in range(4):
                            last = nc.vector.max_index(top_at[:, q, :], top[:, q, :], logits[:, q, :])
                        last.then_inc(chain, 1)
                        dve.wait_ge(chain, base + 5)
                        nc.vector.tensor_copy(at[:, :, :], top_at[:, :, 0:2]).then_inc(chain, 1)
                        dve.wait_ge(sig_ready, j + 1)
                        nc.vector.tensor_tensor(total[:, :], sig[:, :, 0], sig[:, :, 1], ALU.add).then_inc(chain, 1)
                        dve.wait_ge(chain, base + 7)
                        nc.vector.tensor_scalar(total[:, :], total[:, :], 1e-10, None, ALU.add).then_inc(chain, 1)
                        dve.wait_ge(chain, base + 8)
                        nc.vector.reciprocal(total[:, :], total[:, :]).then_inc(chain, 1)
                        dve.wait_ge(chain, base + 9)
                        nc.vector.tensor_tensor(gates[:, :, :], sig[:, :, :],
                                                total[:, :].unsqueeze(2).to_broadcast([P, 4, 2]), ALU.mult)\
                          .then_inc(chain, 1)
                        dve.wait_ge(chain, base + 10)
                        for w, dst in enumerate((gate1, gate2)):
                            for q in range(4):
                                last = nc.vector.tensor_scalar(dst[:, q, :], iota8[:, :], at[:, q, w:w + 1],
                                                               gates[:, q, w:w + 1], ALU.is_equal, ALU.mult)
                            last.then_inc(chain, 1)
                        dve.wait_ge(chain, base + 12)
                        nc.vector.tensor_tensor(ge[t][:, :, :], gate1[:, :, :], gate2[:, :, :], ALU.add)\
                          .then_inc(chain, 2)

                def stored_before(j, t):
                    return j * 8 - 8 * t

                def add_expert(e, j, t):
                    dve.wait_ge(down_ready, j * EXPERTS + e + 1)
                    if e:
                        dve.wait_ge(added, j * EXPERTS + e)
                    else:
                        dve.wait_ge(chain, j * CHAIN + CHAIN)
                    for q in range(4):
                        last = nc.vector.scalar_tensor_tensor(
                            y[t][:, q, :], down_ps[e % 2][:, q * P:(q + 1) * P], ge[t][:, q, e:e + 1],
                            y[t][:, q, :], ALU.mult, ALU.add)
                    last.then_inc(added, 1)

                def expert(e, j, t, is_last):
                    for c in range(2):
                        m = 2 * e + c
                        dve.wait_ge(sg_ready, j * 16 + m + 1)
                        if known(j, 1) or e:
                            dve.wait_ge(hidden_ready, j * 16 + max(m - 1, 0))
                        nc.vector.tensor_tensor(silu[c][:, :], gu_ps[c][0], sg[c][:, :], ALU.mult)\
                          .then_inc(silu_ready, 1)
                        if (known(j, 1) or e >= 2) and c == 0:
                            dve.wait_ge(down_ready, j * EXPERTS + max(e - 1, 0))
                        dve.wait_ge(silu_ready, j * 16 + m + 1)
                        nc.vector.tensor_tensor(hidden[e % 2][:, c, :], gu_ps[c][1], silu[c][:, :], ALU.mult)\
                          .then_inc(hidden_ready, 1)
                    if e:
                        add_expert(e - 1, j, t)
                    if e == EXPERTS - 1:
                        add_expert(e, j, t)

                run_groups(dve, front, expert)

            @block.tensor
            def _(pe):
                def front(n, j, t):
                    if n == 0:
                        pe.wait_ge(o_staged, j + 1)
                        if known(j, 1):
                            pe.wait_ge(xt_ready, j)
                        for q in range(4):
                            last = nc.tensor.transpose(side_ps[0][:, q * P:(q + 1) * P], o_in[:, q, :], ident[:, :])
                        last.then_inc(o_t_ps, 1)
                    if n == 1:
                        pe.wait_ge(o_t_ready, j + 1)
                        if known(j, 1):
                            pe.wait_ge(top_ready, j)
                        for q in range(4):
                            last = nc.tensor.matmul(side_ps[1][:, q * P:(q + 1) * P], o_t[:, q * P:(q + 1) * P],
                                                    wout[:, :], start=True, stop=True)
                        last.then_inc(proj_ps, 1)
                    if n == 2:
                        pe.wait_ge(xn_ready, j + 1)
                        for q in range(4):
                            last = nc.tensor.transpose(side_ps[0][:, q * P:(q + 1) * P], xn[:, q, :], ident[:, :])
                        last.then_inc(xt_ps, 1)
                    if n == 3:
                        pe.wait_ge(xt_ready, j + 1)
                        pe.wait_ge(var_ready, j + 1)
                        for q in range(4):
                            last = nc.tensor.matmul(side_ps[1][:, q * EXPERTS:(q + 1) * EXPERTS],
                                                    xt[t][:, q * P:(q + 1) * P], wr[:, :], start=True, stop=True)
                        last.then_inc(logits_ps, 1)

                def down(e, j):
                    pe.wait_ge(hidden_ready, j * 16 + 2 * e + 2)
                    if known(j, 1) or e >= 2:
                        pe.wait_ge(added, j * EXPERTS + max(e - 1, 0))
                    for q in range(4):
                        for c in range(2):
                            last = nc.tensor.matmul(down_ps[e % 2][:, q * P:(q + 1) * P],
                                                    hidden[e % 2][:, c, q * P:(q + 1) * P], wd[:, e, c, :],
                                                    start=(c == 0), stop=(c == 1))
                    last.then_inc(down_ready, 1)

                def expert(e, j, t, is_last):
                    if e == 0:
                        pe.wait_ge(xt_ready, j + 1)
                    for c in range(2):
                        if known(j, 1) or e:
                            pe.wait_ge(hidden_ready, j * 16 + max(2 * e + c - 1, 0))
                        for w, dst in ((wg, gu_ps[c][0]), (wu, gu_ps[c][1])):
                            last = nc.tensor.matmul(dst, w[:, e, c * P:(c + 1) * P], xt[t][:, :],
                                                    start=True, stop=True)
                        last.then_inc(gu_ready, 1)
                    if e:
                        down(e - 1, j)
                    if e == EXPERTS - 1:
                        down(e, j)

                run_groups(pe, front, expert)


_OUT = ((BATCH, SEQ, DM), "float32")


def kernel(**inputs):
    import numpy as _np
    import concourse.bacc as _bacc
    from concourse import mybir as _mybir
    from concourse.bass_utils import run_bass_kernel_spmd as _run

    nc = _bacc.Bacc("TRN2", target_bir_lowering=False, num_devices=1)
    rel = _np.minimum(_np.arange(1 - SEQ, SEQ + 1, dtype=_np.float32), SEQ - 1)
    rel_log = (_np.sign(rel) * _np.log1p(_np.abs(rel))).astype(_np.float32)
    arrays, args = {}, []

    def give(name, a):
        a = _np.ascontiguousarray(a)
        arrays[name] = a
        args.append(nc.dram_tensor(name, a.shape, _mybir.dt.from_np(a.dtype), kind="ExternalInput").ap())

    for name in ("L0_attn_x", "L0_attn_w_qkv", "L0_attn_b_qkv", "L0_attn_w_out", "L0_attn_b_out",
                 "L0_attn_w1_rpe", "L0_attn_b1_rpe", "L0_attn_w2_rpe", "L0_attn_b2_rpe"):
        give("in_" + name, inputs[name])
    give("in_router", _np.asarray(inputs["L0_ffn_router_w"]).T)
    for name in ("L0_ffn_w_gate", "L0_ffn_w_up", "L0_ffn_w_down"):
        give("in_" + name, inputs[name])
    give("rel_log", rel_log)
    args.append(nc.dram_tensor("out_0", _OUT[0], _mybir.dt.from_np(_np.dtype(_OUT[1])), kind="ExternalOutput").ap())
    build(nc, *args)
    r = _run(nc, [arrays], core_ids=[0])
    return r.results[0]["out_0"]
```

```python
import concourse.bass as bass
from concourse import mybir
from contextlib import ExitStack


FP32 = mybir.dt.float32
BF16 = mybir.dt.bfloat16
U32 = mybir.dt.uint32
ALU = mybir.AluOpType
ACT = mybir.ActivationFunctionType
AX = mybir.AxisListType

BATCH, SEQ, DM = 4, 1024, 128
HEADS, DH = 16, 8
RPE = 32
EXPERTS, HID = 8, 256
P = 128
TILES = BATCH * SEQ // P
CH = SEQ // P
GROUPS = TILES // 4
PLANES = 3
ROWS = 96
SHIFT_ROWS = 2 * CH
KROWS = ROWS + SHIFT_ROWS
TABW = SEQ + SEQ - P
NREL = 2 * SEQ

UNITS = HEADS * BATCH
STEPS = UNITS * CH
LEAD = 12
LAG = 3
NORM_AT, SHIFT_AT, COPY_AT = 4, 6, 7
ADDED = (0, 4)
HALVED = (2,)
BODY = 8 * CH
FIRST = 24
TURNS = (STEPS - FIRST - LEAD) // BODY
LOOP_END = FIRST + TURNS * BODY
FRONT_PE = (0, 2, 4, 7)
FRONT_DVE = (0, 2, 3, 7)
FRONT_ACT = (0, 1, 4, 7)


def exists(kind, g):
    n = g // CH
    if kind == "max":
        return 0 <= g + LEAD < STEPS
    if kind == "exp":
        return 0 <= g < STEPS
    if kind == "pv":
        return 0 <= g - LAG < STEPS
    if kind == "norm":
        return g % CH == NORM_AT and 1 <= n <= UNITS
    return g % CH == SHIFT_AT and 0 <= n + 1 < UNITS


def wait_apart(engine, semaphore, value, passed):
    engine.wait_ge(semaphore, value)
    engine.sem_inc(passed, 1)


def build(nc, x, w_qkv, b_qkv, w_out, b_out, w1, b1, w2, b2, router_w, w_gate, w_up, w_down, rel_log, out):
    q_planes = nc.dram_tensor("q_planes", [BATCH, HEADS, PLANES * DH, SEQ], BF16).ap()
    k_planes = nc.dram_tensor("k_planes", [BATCH, HEADS, (2 * PLANES - 1) * DH, SEQ], BF16).ap()
    bias_rows = nc.dram_tensor("bias_rows", [2, HEADS, NREL], FP32).ap()

    with ExitStack() as ctx:
        def sb(name, shape, dt=FP32):
            return ctx.enter_context(nc.sbuf_tensor(name, shape, dt))

        xall = sb("xall", [P, TILES, DM])
        vall = sb("vall", [P, TILES, DM])
        oall = sb("oall", [P, TILES, DM])
        wg = sb("wg", [P, EXPERTS, HID])
        wu = sb("wu", [P, EXPERTS, HID])
        wd = sb("wd", [P, EXPERTS, 2, DM])
        wout = sb("wout", [P, DM])
        bout = sb("bout", [P, DM])
        wr = sb("wr", [P, EXPERTS])
        ident = sb("ident", [P, P])
        identb = sb("identb", [P, P], BF16)
        mirror = sb("mirror", [P, P])
        iota8 = sb("iota8", [P, EXPERTS])
        minus_half = sb("minus_half", [P, TILES])
        area = sb("area", [P, 8 * SEQ + 4 * TABW])
        ps = ctx.enter_context(nc.psum_tensor("ps", [P, 8, 512], FP32))

        qst = [sb(f"qst{i}", [P, SEQ], BF16) for i in range(4)]
        kst = [sb(f"kst{i}", [P, SEQ], BF16) for i in range(4)]
        vst = [sb(f"vst{i}", [P, CH, 32]) for i in range(2)]
        shifts = sb("shifts", [P, CH * SHIFT_ROWS], BF16)

        prepare(nc, x, w_qkv, b_qkv, w_out, b_out, w1, b1, w2, b2, router_w, w_gate, w_up, w_down, rel_log,
                q_planes, k_planes, bias_rows, xall, vall, wg, wu, wd, wout, bout, wr, ident, identb, mirror, iota8,
                minus_half, area, ps, qst, kst, vst, shifts)
        attend(nc, q_planes, k_planes, bias_rows, vall, oall, ident, identb, area, ps, qst, kst, vst, shifts)
        finish(nc, out, xall, oall, wg, wu, wd, wout, bout, wr, ident, iota8, minus_half, ps)


def prepare(nc, x, w_qkv, b_qkv, w_out, b_out, w1, b1, w2, b2, router_w, w_gate, w_up, w_down, rel_log,
            q_planes, k_planes, bias_rows, xall, vall, wg, wu, wd, wout, bout, wr, ident, identb, mirror, iota8,
            minus_half, area, ps, qst, kst, vst, shifts):
    with ExitStack() as ctx:
        def sb(name, shape, dt=FP32):
            return ctx.enter_context(nc.sbuf_tensor(name, shape, dt))

        def sem(name):
            return ctx.enter_context(nc.semaphore(name))

        half = PLANES * TILES * P // 2
        qp = area[:, 0:half].bitcast(BF16).rearrange("p (j t) -> p j t", j=PLANES)
        kp = area[:, half:2 * half].bitcast(BF16).rearrange("p (j t) -> p j t", j=PLANES)
        wqkv = sb("wqkv", [P, 3 * DM])
        bq = sb("bq", [P, 1])
        bk = sb("bk", [P, 1])
        bv = sb("bv", [P, DM])
        rel = sb("rel", [RPE, NREL])
        hid = sb("hid", [RPE, NREL])
        w1c = sb("w1c", [RPE, 1])
        b1c = sb("b1c", [RPE, 1])
        w2s = sb("w2s", [RPE, HEADS])
        b2c = sb("b2c", [HEADS, 1])
        bias = sb("bias", [HEADS, NREL])
        ebias = sb("ebias", [HEADS, NREL])
        bmax = sb("bmax", [HEADS, 1])
        stats = sb("stats", [P, TILES, 6])
        mv = sb("mv", [P, TILES, 2])
        rstd = sb("rstd", [P, TILES])
        xn = sb("xn", [P, 4, DM])
        xt = sb("xt", [P, 512])
        xt_rev = sb("xt_rev", [P, 512])
        qf = sb("qf", [P, 512])
        kf = sb("kf", [P, 512])
        kr = sb("kr", [P, 512])
        qr = sb("qr", [P, 512])

        x_loaded = sem("x_loaded")
        small_loaded = sem("small_loaded")
        weights_loaded = sem("weights_loaded")
        const_ready = sem("const_ready")
        v_zeroed = sem("v_zeroed")
        stats_ready = sem("stats_ready")
        aggr_ready = sem("aggr_ready")
        rstd_ready = sem("rstd_ready")
        hidden_ready = sem("hidden_ready")
        bias_ps = sem("bias_ps")
        bias_chain = sem("bias_chain")
        bias_ready = sem("bias_ready")
        ebias_ready = sem("ebias_ready")
        bias_stored = sem("bias_stored")
        xn_ready = sem("xn_ready")
        xt_ps = sem("xt_ps")
        xt_ready = sem("xt_ready")
        qkv_ps = sem("qkv_ps")
        kf_ready = sem("kf_ready")
        v_ready = sem("v_ready")
        split = sem("split")
        ksplit = sem("ksplit")
        planes_stored = sem("planes_stored")
        pool_waits = sem("pool_waits1")

        xt_bank, q_bank, k_bank, v_bank, xt_rev_bank = (ps[:, i, :] for i in range(5))

        with nc.Block() as block:
            @block.sync
            def _(sp):
                sp.dma_start(rel[:, :], rel_log.partition_broadcast(RPE)).then_inc(small_loaded, 16)
                for dst, src in ((w1c, w1.rearrange("a j -> j a")), (b1c, b1.rearrange("(j a) -> j a", a=1)),
                                 (w2s, w2), (b2c, b2.rearrange("(h a) -> h a", a=1)),
                                 (wqkv, w_qkv), (bq, b_qkv[0:DM].rearrange("(c a) -> c a", a=1)),
                                 (bk, b_qkv[DM:2 * DM].rearrange("(c a) -> c a", a=1)),
                                 (bv, b_qkv[2 * DM:3 * DM].partition_broadcast(P))):
                    sp.dma_start(dst[:, :], src).then_inc(small_loaded, 16)
                for dst, src in ((wout[:, :], w_out), (bout[:, :], b_out.partition_broadcast(P)),
                                 (wr[:, :], router_w), (wg[:, :, :], w_gate.rearrange("e d h -> d e h")),
                                 (wu[:, :, :], w_up.rearrange("e d h -> d e h")),
                                 (wd[:, :, :, :], w_down.rearrange("e (c h) d -> h e c d", c=2))):
                    sp.dma_start(dst, src).then_inc(weights_loaded, 16)
                sp.wait_ge(bias_ready, 1)
                sp.dma_start(bias_rows[0, :, :], bias[:, :]).then_inc(bias_stored, 16)
                sp.wait_ge(ebias_ready, 1)
                sp.dma_start(bias_rows[1, :, :], ebias[:, :]).then_inc(bias_stored, 16)
                with sp.Fori(0, BATCH) as b:
                    sp.wait_ge(split, b * 10 + 10)
                    for j in range(PLANES):
                        sp.dma_start(q_planes[b, :, j * DH:(j + 1) * DH, :], qp[:, j, bass.ds(b * SEQ, SEQ)])\
                          .then_inc(planes_stored, 16)
                    sp.wait_ge(ksplit, b * 8 + 8)
                    for j in range(2 * PLANES - 1):
                        sp.dma_start(k_planes[b, :, j * DH:(j + 1) * DH, :],
                                     kp[:, j % PLANES, bass.ds(b * SEQ, SEQ)]).then_inc(planes_stored, 16)
                sp.wait_ge(bias_stored, 32)
                sp.wait_ge(planes_stored, BATCH * (3 * PLANES - 1) * 16)
                sp.wait_ge(weights_loaded, 6 * 16)

            @block.gpsimd
            def _(pool):
                pool.memset(ident[:, :], 0.0).then_inc(const_ready, 1)
                pool.memset(identb[:, :], 0.0).then_inc(const_ready, 1)
                pool.memset(minus_half[:, :], -0.5).then_inc(const_ready, 1)
                pool.iota(iota8[:, :], pattern=[[1, EXPERTS]], base=0, channel_multiplier=0,
                          allow_small_or_imprecise_dtypes=True).then_inc(const_ready, 1)
                pool.memset(mirror[:, :], 0.0).then_inc(const_ready, 1)
                pool.wait_ge(const_ready, 5)
                for m in (ident, identb):
                    pool.affine_select(out=m[:, :], in_=m[:, :], compare_op=ALU.not_equal, fill=1.0, base=0,
                                       pattern=[[-1, P]], channel_multiplier=1).then_inc(const_ready, 1)
                pool.affine_select(out=mirror[:, :], in_=mirror[:, :], compare_op=ALU.not_equal, fill=1.0,
                                   base=1 - P, pattern=[[1, P]], channel_multiplier=1).then_inc(const_ready, 1)
                pool.wait_ge(aggr_ready, 1)
                pool.tensor_scalar(rstd[:, :], mv[:, :, 1], 1e-5, None, ALU.add).then_inc(rstd_ready, 1)
                pool.wait_ge(rstd_ready, 1)
                pool.tensor_tensor(rstd[:, :], rstd[:, :], minus_half[:, :], ALU.pow).then_inc(rstd_ready, 1)

                def split_k(j, side):
                    here = bass.ds((j + 1 - 2 * side) * 512, 512)
                    pool.wait_ge(kf_ready, j + 1)
                    pool.tensor_copy(kp[:, 0, here], kf[:, :]).then_inc(ksplit, 1)
                    wait_apart(pool, ksplit, j * 4 + 1, pool_waits)
                    pool.tensor_tensor(kr[:, :], kf[:, :], kp[:, 0, here], ALU.subtract).then_inc(ksplit, 1)
                    pool.wait_ge(ksplit, j * 4 + 2)
                    pool.tensor_copy(kp[:, 1, here], kr[:, :]).then_inc(ksplit, 1)
                    wait_apart(pool, ksplit, j * 4 + 3, pool_waits)
                    pool.tensor_tensor(kp[:, 2, here], kr[:, :], kp[:, 1, here], ALU.subtract).then_inc(ksplit, 1)

                with pool.Fori(0, BATCH) as b:
                    for side in range(2):
                        split_k(b * 2 + side, side)

            @block.scalar
            def _(act):
                for b in range(BATCH):
                    act.dma_start(xall[:, b * CH:(b + 1) * CH, :], x[b].rearrange("(c p) d -> p c d", p=P))\
                       .then_inc(x_loaded, 16)
                act.wait_ge(small_loaded, 9 * 16)
                nc.scalar.activation(hid[:, :], rel[:, :], ACT.Relu, bias=b1c[:, :], scale=w1c[:, :])\
                  .then_inc(hidden_ready, 1)
                act.wait_ge(bias_ready, 1)
                nc.scalar.activation(ebias[:, :], bias[:, :], ACT.Exp).then_inc(ebias_ready, 1)
                with act.Fori(0, GROUPS) as j:
                    act.wait_ge(xt_ps, j + 1)
                    nc.scalar.copy(xt[:, :], xt_bank)
                    nc.scalar.copy(xt_rev[:, :], xt_rev_bank).then_inc(xt_ready, 1)

            @block.vector
            def _(dve):
                nc.vector.memset(shifts[:, :], 0.0)
                for i in range(4):
                    nc.vector.memset(qst[i][64:ROWS, :], 0.0)
                    nc.vector.memset(kst[i][64:ROWS, :], 0.0)
                    nc.vector.memset(kst[i][ROWS:KROWS, :], 1.0)
                nc.vector.memset(vst[0][:, :, :], 0.0)
                nc.vector.memset(vst[1][:, :, :], 0.0).then_inc(v_zeroed, 1)
                dve.wait_ge(v_zeroed, 1)
                for i in range(2):
                    nc.vector.memset(vst[i][:, :, DH:DH + 1], 1.0)
                dve.wait_ge(bias_ps, 1)
                nc.vector.tensor_scalar(bias[:, :], ps[0:HEADS, 4:8, :].rearrange("h a b -> h (a b)"), b2c[:, :], None,
                                        ALU.add).then_inc(bias_chain, 1)
                dve.wait_ge(bias_chain, 1)
                nc.vector.reduce_max(bmax[:, :], bias[:, :], AX.X).then_inc(bias_chain, 1)
                dve.wait_ge(bias_chain, 2)
                nc.vector.tensor_scalar(bias[:, :], bias[:, :], bmax[:, :], None, ALU.subtract).then_inc(bias_ready, 1)
                dve.wait_ge(x_loaded, BATCH * 16)
                with dve.Fori(0, GROUPS) as j:
                    for q in range(4):
                        nc.vector.bn_stats(stats[:, bass.ds(j * 4 + q, 1), :].rearrange("p a s -> p (a s)"),
                                           xall[:, bass.ds(j * 4 + q, 1), :].rearrange("p a s -> p (a s)"))\
                          .then_inc(stats_ready, 1)
                dve.wait_ge(stats_ready, TILES)
                for tile in range(TILES):
                    last = nc.vector.bn_aggr(mv[:, tile, :], stats[:, tile, :])
                last.then_inc(aggr_ready, 1)
                dve.wait_ge(aggr_ready, 1)
                dve.wait_ge(rstd_ready, 2)

                def normalise(j):
                    for q in range(4):
                        tile = bass.ds(j * 4 + q, 1)
                        last = nc.vector.tensor_scalar(
                            xn[:, q, :], xall[:, tile, :].rearrange("p a s -> p (a s)"),
                            mv[:, tile, 0], rstd[:, tile], ALU.subtract, ALU.mult)
                    last.then_inc(xn_ready, 1)

                def split_q(j, side):
                    here = bass.ds(j * 512, 512)
                    dve.wait_ge(qkv_ps, j + 1)
                    nc.vector.tensor_scalar(qf[:, :], q_bank, bq[:, :], float(DH) ** -0.5, ALU.add, ALU.mult)\
                      .then_inc(split, 1)
                    if not isinstance(j, int) or j:
                        dve.wait_ge(ksplit, j * 4)
                    nc.vector.tensor_scalar(kf[:, :], k_bank, bk[:, :], None, ALU.add).then_inc(kf_ready, 1)
                    nc.vector.tensor_tensor(vall[:, bass.ds((j + 1 - 2 * side) * 4, 4), :], v_bank.rearrange("p (q c) -> p q c", q=4),
                                            bv[:, :].unsqueeze(1).to_broadcast([P, 4, DM]), ALU.add)\
                      .then_inc(v_ready, 1)
                    dve.wait_ge(split, j * 5 + 1)
                    nc.vector.tensor_copy(qp[:, 0, here], qf[:, :]).then_inc(split, 1)
                    dve.wait_ge(split, j * 5 + 2)
                    nc.vector.tensor_tensor(qr[:, :], qf[:, :], qp[:, 0, here], ALU.subtract).then_inc(split, 1)
                    dve.wait_ge(split, j * 5 + 3)
                    nc.vector.tensor_copy(qp[:, 1, here], qr[:, :]).then_inc(split, 1)
                    dve.wait_ge(split, j * 5 + 4)
                    nc.vector.tensor_tensor(qp[:, 2, here], qr[:, :], qp[:, 1, here], ALU.subtract)\
                      .then_inc(split, 1)

                def step(j, side):
                    dve.wait_ge(xt_ps, j + 1)
                    normalise(j + 1)
                    split_q(j, side)

                normalise(0)
                for side in range(2):
                    step(side, side)
                with dve.Fori(1, BATCH - 1) as b:
                    for side in range(2):
                        step(b * 2 + side, side)
                dve.wait_ge(xt_ps, GROUPS - 1)
                normalise(GROUPS - 1)
                split_q(GROUPS - 2, 0)
                split_q(GROUPS - 1, 1)

            @block.tensor
            def _(pe):
                pe.wait_ge(hidden_ready, 1)
                for i in range(4):
                    last = nc.tensor.matmul(ps[0:HEADS, 4 + i, :], w2s[:, :], hid[:, i * 512:(i + 1) * 512],
                                            start=True, stop=True)
                last.then_inc(bias_ps, 1)
                pe.wait_ge(bias_chain, 1)
                pe.wait_ge(const_ready, 8)
                pe.wait_ge(small_loaded, 9 * 16)

                def project(j, first):
                    pe.wait_ge(xn_ready, j + 1)
                    if not first:
                        pe.wait_ge(xt_ready, j)
                    for q in range(4):
                        last = nc.tensor.transpose(xt_bank[:, q * P:(q + 1) * P], xn[:, q, :], ident[:, :])
                        last = nc.tensor.transpose(xt_rev_bank[:, (3 - q) * P:(4 - q) * P], xn[:, q, :],
                                                   mirror[:, :])
                    last.then_inc(xt_ps, 1)
                    pe.wait_ge(xt_ready, j + 1)
                    if not first:
                        pe.wait_ge(v_ready, j)
                    nc.tensor.matmul(q_bank, wqkv[:, 0:DM], xt[:, :], start=True, stop=True)
                    nc.tensor.matmul(k_bank, wqkv[:, DM:2 * DM], xt_rev[:, :], start=True, stop=True)
                    for q in range(4):
                        last = nc.tensor.matmul(v_bank[:, q * P:(q + 1) * P], xt_rev[:, q * P:(q + 1) * P],
                                                wqkv[:, 2 * DM:3 * DM], start=True, stop=True)
                    last.then_inc(qkv_ps, 1)

                project(0, True)
                with pe.Fori(1, GROUPS) as j:
                    project(j, False)


def attend(nc, q_planes, k_planes, bias_rows, vall, oall, ident, identb, area, ps, qst, kst, vst, shifts):
    with ExitStack() as ctx:
        def sb(name, shape, dt=FP32):
            return ctx.enter_context(nc.sbuf_tensor(name, shape, dt))

        def sem(name):
            return ctx.enter_context(nc.semaphore(name))

        prob = [area[:, k * SEQ:(k + 1) * SEQ] for k in range(CH)]
        tab0 = CH * SEQ
        bias_tab = [area[:, tab0 + i * TABW:tab0 + (i + 1) * TABW] for i in range(2)]
        mul_tab = [area[:, tab0 + (2 + i) * TABW:tab0 + (3 + i) * TABW] for i in range(2)]
        row_max = [sb(f"row_max{i}", [P, CH]) for i in range(2)]
        ot_sb = [sb(f"ot_sb{i}", [P, 256]) for i in range(2)]
        rden = [sb(f"rden{i}", [P, 2, 4]) for i in range(2)]

        max_ps = [ps[:, 2 * i:2 * i + 2, :].rearrange("p a b -> p (a b)") for i in range(2)]
        exp_ps = [ps[:, 4 + h, :] for h in range(2)]
        ot_ps = [ps[:, 6 + i, 0:256] for i in range(2)]
        norm_in = [ps[:, 6 + i, 256:512] for i in range(2)]
        shift_rows = [ps[ROWS:KROWS, 6 + i, :].bitcast(BF16) for i in range(2)]

        qk_loaded = [sem(f"qk_loaded{i}") for i in range(4)]
        bias_tab_loaded = [sem(f"bias_tab_loaded{i}") for i in range(2)]
        mul_tab_loaded = [sem(f"mul_tab_loaded{i}") for i in range(2)]
        max_scores = sem("max_scores")
        exp_scores = sem("exp_scores")
        shift_ps = sem("shift_ps")
        norm_ps = sem("norm_ps")
        pv_done = sem("pv_done")
        max_done = sem("max_done")
        shifts_high = sem("shifts_high")
        shifts_ready = sem("shifts_ready")
        bias_added = sem("bias_added")
        recip_done = sem("recip_done")
        dve_waits = sem("dve_waits2")
        norm_done = sem("norm_done")
        shift_copied = sem("shift_copied")
        v_staged = sem("v_staged")
        exp_done = sem("exp_done")
        ot_copied = sem("ot_copied")
        bias_multiplied = sem("bias_multiplied")

        def count_steps(r, i, more=0):
            return i * BODY + (r + more)

        def count_halves(r, i, more):
            return i * (2 * BODY) + (2 * r + more)

        def count_units(r, i, more=0, per=1):
            return i * (BODY // CH * per) + (r // CH + more) * per

        def run_steps(engine, step):
            for g in range(-LEAD, FIRST):
                step(g, 0, g)
            with engine.Fori(0, TURNS) as i:
                for r in range(FIRST, FIRST + BODY):
                    step(r, i, r)
            for g in range(LOOP_END, STEPS + CH):
                step(g, 0, g)

        def added_halves(k):
            return 2 if k in ADDED else 1 if k in HALVED else 0

        added_before = [sum(added_halves(c) for c in range(k)) for k in range(CH + 1)]
        multiplied_before = [sum(1 for c in range(k) if c not in ADDED) for k in range(CH + 1)]

        with nc.Block() as block:
            @block.sync
            def _(sp):
                def load_tabs(h, turn):
                    for row, tab, loaded in ((0, bias_tab, bias_tab_loaded), (1, mul_tab, mul_tab_loaded)):
                        at = bias_rows[row, h, 0:TABW]
                        sp.dma_start(tab[turn], bass.AP(at.tensor, at.offset, [[1, P], [1, TABW]]))\
                          .then_inc(loaded[turn], 16)

                def load_unit(u, i):
                    head, b, buf = i * 2 + u // BATCH, u % BATCH, u % 4
                    if u >= 4:
                        sp.wait_ge(exp_scores, i * (2 * BODY) + (u - 3) * (2 * CH))
                    for n in range(PLANES):
                        rows = slice(n * PLANES * DH, (n + 1) * PLANES * DH)
                        sp.dma_start(qst[buf][rows, :], q_planes[b, head, :, :]).then_inc(qk_loaded[buf], 16)
                        sp.dma_start(kst[buf][rows, :], k_planes[b, head, n * DH:(n + PLANES) * DH, :])\
                          .then_inc(qk_loaded[buf], 16)

                def unit(u, i):
                    h, turn = u // BATCH, u // BATCH % 2
                    if u % BATCH == 0 and u >= 8:
                        sp.wait_ge(pv_done, i * BODY + (h - 1) * BATCH * CH)
                        load_tabs(i * 2 + h, turn)
                    load_unit(u, i)

                load_tabs(0, 0)
                for u in range(0, 4):
                    load_unit(u, 0)
                load_tabs(1, 1)
                for u in range(4, 8):
                    unit(u, 0)
                with sp.Fori(0, UNITS // 8 - 1) as i:
                    for u in range(8, 16):
                        unit(u, i)

            @block.gpsimd
            def _(pool):
                def step(r, i, g):
                    k, turn = r % CH, r // (BATCH * CH) % 2
                    if not exists("exp", g) or k in ADDED:
                        return
                    if r % (BATCH * CH) == min(set(range(CH)) - set(ADDED)):
                        pool.wait_ge(mul_tab_loaded[turn], i * 16 + (r // (2 * BATCH * CH) + 1) * 16)
                    pool.wait_ge(exp_done, count_halves(r, i, 2))
                    here = slice(512, SEQ) if k in HALVED else slice(0, SEQ)
                    pool.tensor_tensor(prob[k][:, here], prob[k][:, here], mul_tab[turn][:, k * P:k * P + SEQ][:, here],
                                       ALU.mult).then_inc(bias_multiplied, 1)

                run_steps(pool, step)

            @block.scalar
            def _(act):
                def step(r, i, g):
                    k, u = r % CH, r // CH
                    if k == COPY_AT and exists("shift", g - k + SHIFT_AT):
                        act.wait_ge(shift_ps, count_units(r, i, 2))
                        nc.scalar.copy(qst[(u + 1) % 4][ROWS:KROWS, :], shift_rows[(u + 1) % 2])\
                          .then_inc(shift_copied, 1)
                    if exists("exp", g) and k == 0:
                        if u >= 2:
                            act.wait_ge(pv_done, count_units(r, i, -1, CH))
                        b, h8 = u % BATCH, i * (2 * DH) + u // BATCH * DH
                        nc.scalar.copy(vst[u % 2][:, :, 0:DH], vall[:, b * CH:(b + 1) * CH, bass.ds(h8, DH)])\
                          .then_inc(v_staged, 1)
                    if exists("exp", g):
                        if r >= CH:
                            act.wait_ge(pv_done, count_steps(r, i, 1 - CH))
                        for h in range(2):
                            if h < added_halves(k):
                                act.wait_ge(bias_added, count_units(r, i, 0, added_before[CH])
                                            + (added_before[k] + h + 1))
                            else:
                                act.wait_ge(exp_scores, count_halves(r, i, h + 1))
                            nc.scalar.activation(prob[k][:, h * 512:(h + 1) * 512], exp_ps[h], ACT.Exp)\
                              .then_inc(exp_done, 1)
                    if k == LAG and u >= 1 and exists("norm", g - k + NORM_AT):
                        act.wait_ge(pv_done, count_units(r, i, 0, CH))
                        if u >= 3:
                            act.wait_ge(norm_ps, count_units(r, i, -2))
                        nc.scalar.copy(ot_sb[(u - 1) % 2][:, :], ot_ps[(u - 1) % 2]).then_inc(ot_copied, 1)

                run_steps(act, step)

            @block.vector
            def _(dve):
                def step(r, i, g):
                    k, u = r % CH, r // CH
                    if exists("exp", g):
                        turn = r // (BATCH * CH) % 2
                        for h in range(added_halves(k)):
                            at = k * P + h * 512
                            dve.wait_ge(exp_scores, count_halves(r, i, h + 1))
                            nc.vector.tensor_tensor(exp_ps[h], exp_ps[h], bias_tab[turn][:, at:at + 512], ALU.add)\
                              .then_inc(bias_added, 1)
                    if exists("max", g):
                        a = r + LEAD
                        ka, ua, turn = a % CH, a // CH, a // (BATCH * CH) % 2
                        if a % (BATCH * CH) == 0:
                            dve.wait_ge(bias_tab_loaded[turn], i * 16 + (a // (2 * BATCH * CH) + 1) * 16)
                        if ka == 0 and ua >= 2:
                            dve.wait_ge(shifts_ready, count_units(a, i, -1))
                        wait_apart(dve, max_scores, count_steps(a, i, 1), dve_waits)
                        nc.vector.tensor_tensor_reduce(
                            out=max_ps[k % 2], in0=max_ps[k % 2],
                            in1=bias_tab[turn][:, ka * P:ka * P + SEQ], scale=1.0,
                            scalar=-3.0e38, op0=ALU.add, op1=ALU.max,
                            accum_out=row_max[ua % 2][:, ka:ka + 1]).then_inc(max_done, 1)
                    if exists("max", g) and ka == CH - 1:
                        dve.wait_ge(max_done, count_steps(a, i, 1))
                        if ua >= 1:
                            dve.wait_ge(shift_ps, count_units(a, i))
                        nc.vector.tensor_scalar(shifts[:, 0:CH * SHIFT_ROWS:SHIFT_ROWS + 1], row_max[ua % 2][:, :],
                                                -1.0, None, ALU.mult).then_inc(shifts_high, 1)
                        dve.wait_ge(shifts_high, count_units(a, i, 1))
                        nc.vector.scalar_tensor_tensor(shifts[:, CH:CH * SHIFT_ROWS:SHIFT_ROWS + 1],
                                                       row_max[ua % 2][:, :], -1.0,
                                                       shifts[:, 0:CH * SHIFT_ROWS:SHIFT_ROWS + 1],
                                                       ALU.mult, ALU.subtract).then_inc(shifts_ready, 1)
                    if exists("norm", g):
                        dve.wait_ge(norm_ps, count_units(r, i))
                        o = norm_in[(u - 1) % 2].rearrange("p (i j c) -> p i j c", i=2, j=4)
                        nc.vector.reciprocal(rden[u % 2][:, :, :], o[:, :, :, DH]).then_inc(recip_done, 1)
                        dve.wait_ge(recip_done, count_units(r, i))
                        b, h8 = (u - 1) % BATCH, i * (2 * DH) + (u - 1) // BATCH * DH
                        dst = oall[:, b * CH:(b + 1) * CH, bass.ds(h8, DH)].rearrange("p (j i) d -> p i j d", j=4)
                        nc.vector.tensor_tensor(dst, o[:, :, :, 0:DH],
                                                rden[u % 2][:, :, :].unsqueeze(3).to_broadcast([P, 2, 4, DH]), ALU.mult)\
                          .then_inc(norm_done, 1)

                run_steps(dve, step)
                dve.wait_ge(norm_done, UNITS)

            @block.tensor
            def _(pe):
                def step(r, i, g):
                    k, u = r % CH, r // CH
                    if exists("max", g):
                        a = r + LEAD
                        ka, ua = a % CH, a // CH
                        if ka == 0:
                            pe.wait_ge(qk_loaded[ua % 4], i * (2 * 96) + (ua // 4 + 1) * 96)
                        if g + LEAD >= 2:
                            pe.wait_ge(max_done, count_steps(a, i, -1))
                        q, kk, dst = qst[ua % 4], kst[ua % 4], max_ps[k % 2]
                        for c in range(2):
                            last = nc.tensor.matmul(dst[:, c * 512:(c + 1) * 512], q[0:ROWS, ka * P:(ka + 1) * P],
                                                    kk[0:ROWS, c * 512:(c + 1) * 512], start=True, stop=True)
                        last.then_inc(max_scores, 1)
                    if exists("exp", g):
                        if k == 0:
                            pe.wait_ge(shift_copied, count_units(r, i, 1))
                        for h in range(2):
                            if g >= 1:
                                pe.wait_ge(exp_done, count_halves(r, i, h - 1))
                            nc.tensor.matmul(exp_ps[h], kst[u % 4][0:KROWS, k * P:(k + 1) * P],
                                             qst[u % 4][0:KROWS, h * 512:(h + 1) * 512], start=True, stop=True)\
                              .then_inc(exp_scores, 1)
                    if exists("pv", g):
                        c = r - LAG
                        kc, uc = c % CH, c // CH
                        if kc == 0:
                            pe.wait_ge(v_staged, count_units(c, i, 1))
                        if kc in ADDED:
                            pe.wait_ge(exp_done, count_halves(c, i, 2))
                        else:
                            pe.wait_ge(bias_multiplied, count_units(c, i, 0, multiplied_before[CH])
                                       + (multiplied_before[kc] + 1))
                        for j in range(4):
                            last = nc.tensor.matmul(ot_ps[uc % 2][32 * j:32 * j + 32, :], vst[uc % 2][:, kc, :],
                                                    prob[kc][:, 256 * j:256 * j + 256],
                                                    start=(kc == 0), stop=(kc == CH - 1))
                        last.then_inc(pv_done, 1)
                    if exists("norm", g):
                        pe.wait_ge(ot_copied, count_units(r, i))
                        for c in range(2):
                            last = nc.tensor.transpose(norm_in[(u - 1) % 2][:, c * P:(c + 1) * P],
                                                       ot_sb[(u - 1) % 2][:, c * P:(c + 1) * P], ident[:, :])
                        last.then_inc(norm_ps, 1)
                    if exists("shift", g):
                        if g >= CH:
                            pe.wait_ge(norm_done, count_units(r, i))
                        pe.wait_ge(shifts_ready, count_units(r, i, 2))
                        for c in range(CH):
                            last = nc.tensor.transpose(shift_rows[(u + 1) % 2][:, c * P:(c + 1) * P],
                                                       shifts[:, c * SHIFT_ROWS:(c + 1) * SHIFT_ROWS], identb[:, :])
                        last.then_inc(shift_ps, 1)

                run_steps(pe, step)


def finish(nc, out, xall, oall, wg, wu, wd, wout, bout, wr, ident, iota8, minus_half, ps):
    out_t = out.rearrange("b (c p) d -> p (b c) d", p=P)
    with ExitStack() as ctx:
        def sb(name, shape, dt=FP32):
            return ctx.enter_context(nc.sbuf_tensor(name, shape, dt))

        def sem(name):
            return ctx.enter_context(nc.semaphore(name))

        o_in = sb("o_in", [P, 4, DM])
        o_t = sb("o_t", [P, 512])
        y = [sb(f"y{i}", [P, 4, DM]) for i in range(2)]
        stats = sb("stats2", [P, 4, 6])
        mv = sb("mv2", [P, 4, 2])
        rstd = sb("rstd2", [P, 4])
        xn = sb("xn2", [P, 4, DM])
        xt = [sb(f"xt{i}", [P, 512]) for i in range(2)]
        logits = sb("logits", [P, 4, EXPERTS])
        top = sb("top", [P, 4, EXPERTS])
        top_at = sb("top_at", [P, 4, EXPERTS], U32)
        at = sb("at", [P, 4, 2])
        sig = sb("sig", [P, 4, 2])
        total = sb("total", [P, 4])
        gates = sb("gates", [P, 4, 2])
        gate1 = sb("gate1", [P, 4, EXPERTS])
        gate2 = sb("gate2", [P, 4, EXPERTS])
        ge = [sb(f"ge{i}", [P, 4, EXPERTS]) for i in range(2)]
        sg = [sb(f"sg{i}", [P, 512]) for i in range(2)]
        silu = [sb(f"silu{i}", [P, 512]) for i in range(2)]
        hidden = [sb(f"hidden{i}", [P, 2, 512]) for i in range(2)]

        gu_ps = [(ps[:, 2 * c, :], ps[:, 2 * c + 1, :]) for c in range(2)]
        down_ps = [ps[:, 4 + i, :] for i in range(2)]
        side_ps = [ps[:, 6 + i, :] for i in range(2)]

        o_staged = sem("o_staged")
        o_t_ps = sem("o_t_ps")
        o_t_ready = sem("o_t_ready")
        proj_ps = sem("proj_ps")
        var_ready = sem("var_ready")
        rstd_ready = sem("rstd_ready2")
        xn_ready = sem("xn_ready2")
        xt_ps = sem("xt_ps2")
        xt_ready = sem("xt_ready2")
        logits_ps = sem("logits_ps")
        top_ready = sem("top_ready")
        sig_ready = sem("sig_ready")
        chain = sem("chain")
        pow_chain = sem("pow_chain")
        dve_waits = sem("dve_waits3")
        pool_waits = sem("pool_waits3")
        gu_ready = sem("gu_ready")
        sg_ready = sem("sg_ready")
        silu_ready = sem("silu_ready")
        hidden_ready = sem("hidden_ready2")
        down_ready = sem("down_ready")
        added = sem("added")
        stored = [sem(f"stored{i}") for i in range(2)]
        CHAIN = 14

        def run_groups(engine, parts_at, front, expert, tail):
            def group(j, after, t):
                for e in range(EXPERTS):
                    expert(e, j, t)
                    for n in range(4):
                        if e == parts_at[n] and after is not None:
                            front(n, after, 1 - t)

            for n in range(4):
                front(n, 0, 0)
            group(0, 1, 0)
            with engine.Fori(0, GROUPS // 2 - 1) as i:
                for t in (1, 0):
                    group(i * 2 + (2 - t), i * 2 + (3 - t), t)
            group(GROUPS - 1, None, 1)
            tail(GROUPS - 1, 1)

        def known(j, least):
            return not isinstance(j, int) or j >= least

        with nc.Block() as block:
            @block.sync
            def _(sp):
                def store(j, t):
                    sp.wait_ge(added, j * EXPERTS + EXPERTS)
                    sp.dma_start(out_t[:, bass.ds(j * 4, 4), :], y[t][:, :, :]).then_inc(stored[t], 16)

                with sp.Fori(0, GROUPS // 2) as i:
                    for t in range(2):
                        store(i * 2 + t, t)
                for t in range(2):
                    sp.wait_ge(stored[t], GROUPS // 2 * 16)

            @block.gpsimd
            def _(pool):
                with pool.Fori(0, GROUPS) as j:
                    wait_apart(pool, var_ready, j + 1, pool_waits)
                    pool.tensor_scalar(rstd[:, :], mv[:, :, 1], 1e-5, None, ALU.add).then_inc(pow_chain, 1)
                    pool.wait_ge(pow_chain, j + 1)
                    pool.tensor_tensor(rstd[:, :], rstd[:, :], minus_half[:, 0:4], ALU.pow).then_inc(rstd_ready, 1)

            @block.scalar
            def _(act):
                def front(n, j, t):
                    if n == 0:
                        if known(j, 1):
                            act.wait_ge(o_t_ps, j)
                        nc.scalar.copy(o_in[:, :, :], oall[:, bass.ds(j * 4, 4), :]).then_inc(o_staged, 1)
                    if n == 1:
                        act.wait_ge(o_t_ps, j + 1)
                        if known(j, 1):
                            act.wait_ge(proj_ps, j)
                        nc.scalar.copy(o_t[:, :], side_ps[0]).then_inc(o_t_ready, 1)
                    if n == 2:
                        act.wait_ge(xt_ps, j + 1)
                        nc.scalar.copy(xt[t][:, :], side_ps[0]).then_inc(xt_ready, 1)
                    if n == 3:
                        act.wait_ge(top_ready, j + 1)
                        nc.scalar.activation(sig[:, :, :], top[:, :, 0:2], ACT.Sigmoid).then_inc(sig_ready, 1)

                def expert(e, j, t):
                    for c in range(2):
                        m = 2 * e + c
                        act.wait_ge(gu_ready, j * 16 + (m + 1))
                        if m >= 2 or known(j, 1):
                            act.wait_ge(silu_ready, j * 16 + (m - 1))
                        nc.scalar.activation(sg[c][:, :], gu_ps[c][0], ACT.Sigmoid).then_inc(sg_ready, 1)

                run_groups(act, FRONT_ACT, front, expert, lambda j, t: None)

            @block.vector
            def _(dve):
                def front(n, j, t):
                    base = j * CHAIN
                    if n == 1:
                        dve.wait_ge(proj_ps, j + 1)
                        if known(j, 2):
                            if isinstance(j, int):
                                dve.wait_ge(stored[t], j // 2 * 16)
                            else:
                                dve.wait_ge(stored[t], stored_before(j, t))
                        nc.vector.tensor_tensor(y[t][:, :, :], side_ps[1].rearrange("p (q c) -> p q c", q=4),
                                                xall[:, bass.ds(j * 4, 4), :], ALU.add).then_inc(chain, 1)
                        dve.wait_ge(chain, base + 1)
                        nc.vector.tensor_tensor(y[t][:, :, :], y[t][:, :, :],
                                                bout[:, :].unsqueeze(1).to_broadcast([P, 4, DM]), ALU.add)\
                          .then_inc(chain, 1)
                        dve.wait_ge(chain, base + 2)
                        for q in range(4):
                            last = nc.vector.bn_stats(stats[:, q, :], y[t][:, q, :])
                        last.then_inc(chain, 1)
                        wait_apart(dve, chain, base + 3, dve_waits)
                        for q in range(4):
                            last = nc.vector.bn_aggr(mv[:, q, :], stats[:, q, :])
                        last.then_inc(var_ready, 1)
                    if n == 2:
                        dve.wait_ge(var_ready, j + 1)
                        dve.wait_ge(rstd_ready, j + 1)
                        for q in range(4):
                            last = nc.vector.tensor_scalar(xn[:, q, :], y[t][:, q, :], mv[:, q, 0:1],
                                                           rstd[:, q:q + 1], ALU.subtract, ALU.mult)
                        last.then_inc(xn_ready, 1)
                    if n == 3:
                        dve.wait_ge(logits_ps, j + 1)
                        nc.vector.tensor_copy(logits[:, :, :], side_ps[1][:, 0:4 * EXPERTS]
                                              .rearrange("p (q e) -> p q e", q=4)).then_inc(chain, 1)
                        wait_apart(dve, chain, base + 4, dve_waits)
                        for q in range(4):
                            last = nc.vector.max(top[:, q, :], logits[:, q, :])
                        last.then_inc(top_ready, 1)
                        wait_apart(dve, top_ready, j + 1, dve_waits)
                        for q in range(4):
                            last = nc.vector.max_index(top_at[:, q, :], top[:, q, :], logits[:, q, :])
                        last.then_inc(chain, 1)
                        dve.wait_ge(chain, base + 5)
                        nc.vector.tensor_copy(at[:, :, :], top_at[:, :, 0:2]).then_inc(chain, 1)
                        dve.wait_ge(sig_ready, j + 1)
                        nc.vector.tensor_tensor(total[:, :], sig[:, :, 0], sig[:, :, 1], ALU.add).then_inc(chain, 1)
                        dve.wait_ge(chain, base + 7)
                        nc.vector.tensor_scalar(total[:, :], total[:, :], 1e-10, None, ALU.add).then_inc(chain, 1)
                        dve.wait_ge(chain, base + 8)
                        nc.vector.reciprocal(total[:, :], total[:, :]).then_inc(chain, 1)
                        dve.wait_ge(chain, base + 9)
                        nc.vector.tensor_tensor(gates[:, :, :], sig[:, :, :],
                                                total[:, :].unsqueeze(2).to_broadcast([P, 4, 2]), ALU.mult)\
                          .then_inc(chain, 1)
                        dve.wait_ge(chain, base + 10)
                        for w, dst in enumerate((gate1, gate2)):
                            for q in range(4):
                                last = nc.vector.tensor_scalar(dst[:, q, :], iota8[:, :], at[:, q, w:w + 1],
                                                               gates[:, q, w:w + 1], ALU.is_equal, ALU.mult)
                            last.then_inc(chain, 1)
                        dve.wait_ge(chain, base + 12)
                        nc.vector.tensor_tensor(ge[t][:, :, :], gate1[:, :, :], gate2[:, :, :], ALU.add)\
                          .then_inc(chain, 2)

                def stored_before(j, t):
                    return j * 8 - 8 * t

                def add_expert(e, j, t):
                    dve.wait_ge(down_ready, j * EXPERTS + (e + 1))
                    if e:
                        dve.wait_ge(added, j * EXPERTS + e)
                    else:
                        dve.wait_ge(chain, j * CHAIN + CHAIN)
                    for q in range(4):
                        last = nc.vector.scalar_tensor_tensor(
                            y[t][:, q, :], down_ps[e % 2][:, q * P:(q + 1) * P], ge[t][:, q, e:e + 1],
                            y[t][:, q, :], ALU.mult, ALU.add)
                    last.then_inc(added, 1)

                def expert(e, j, t):
                    for c in range(2):
                        m = 2 * e + c
                        dve.wait_ge(sg_ready, j * 16 + (m + 1))
                        if m >= 2 or known(j, 1):
                            dve.wait_ge(hidden_ready, j * 16 + (m - 1))
                        nc.vector.tensor_tensor(silu[c][:, :], gu_ps[c][0], sg[c][:, :], ALU.mult)\
                          .then_inc(silu_ready, 1)
                        if c == 0 and (e >= 2 or known(j, 1)):
                            dve.wait_ge(down_ready, j * EXPERTS + (e - 1))
                        dve.wait_ge(silu_ready, j * 16 + (m + 1))
                        nc.vector.tensor_tensor(hidden[e % 2][:, c, :], gu_ps[c][1], silu[c][:, :], ALU.mult)\
                          .then_inc(hidden_ready, 1)
                    if e:
                        add_expert(e - 1, j, t)
                    elif known(j, 1):
                        add_expert(EXPERTS - 1, j - 1, 1 - t)

                run_groups(dve, FRONT_DVE, front, expert, lambda j, t: add_expert(EXPERTS - 1, j, t))

            @block.tensor
            def _(pe):
                def front(n, j, t):
                    if n == 0:
                        pe.wait_ge(o_staged, j + 1)
                        if known(j, 1):
                            pe.wait_ge(xt_ready, j)
                        for q in range(4):
                            last = nc.tensor.transpose(side_ps[0][:, q * P:(q + 1) * P], o_in[:, q, :], ident[:, :])
                        last.then_inc(o_t_ps, 1)
                    if n == 1:
                        pe.wait_ge(o_t_ready, j + 1)
                        if known(j, 1):
                            pe.wait_ge(top_ready, j)
                        for q in range(4):
                            last = nc.tensor.matmul(side_ps[1][:, q * P:(q + 1) * P], o_t[:, q * P:(q + 1) * P],
                                                    wout[:, :], start=True, stop=True)
                        last.then_inc(proj_ps, 1)
                    if n == 2:
                        pe.wait_ge(xn_ready, j + 1)
                        for q in range(4):
                            last = nc.tensor.transpose(side_ps[0][:, q * P:(q + 1) * P], xn[:, q, :], ident[:, :])
                        last.then_inc(xt_ps, 1)
                    if n == 3:
                        pe.wait_ge(xt_ready, j + 1)
                        pe.wait_ge(var_ready, j + 1)
                        for q in range(4):
                            last = nc.tensor.matmul(side_ps[1][:, q * EXPERTS:(q + 1) * EXPERTS],
                                                    xt[t][:, q * P:(q + 1) * P], wr[:, :], start=True, stop=True)
                        last.then_inc(logits_ps, 1)

                def down(e, j, part):
                    if part == 0:
                        pe.wait_ge(hidden_ready, j * 16 + (2 * e + 2))
                        if e >= 2 or known(j, 1):
                            pe.wait_ge(added, j * EXPERTS + (e - 1))
                    for q in range(2 * part, 2 * part + 2):
                        for c in range(2):
                            last = nc.tensor.matmul(down_ps[e % 2][:, q * P:(q + 1) * P],
                                                    hidden[e % 2][:, c, q * P:(q + 1) * P], wd[:, e, c, :],
                                                    start=(c == 0), stop=(c == 1))
                    if part == 1:
                        last.then_inc(down_ready, 1)

                def expert(e, j, t):
                    if e == 0:
                        pe.wait_ge(xt_ready, j + 1)
                    for c in range(2):
                        if e or known(j, 1):
                            pe.wait_ge(hidden_ready, j * 16 + (2 * e + c - 1))
                        for w, dst in ((wg, gu_ps[c][0]), (wu, gu_ps[c][1])):
                            last = nc.tensor.matmul(dst, w[:, e, c * P:(c + 1) * P], xt[t][:, :],
                                                    start=True, stop=True)
                        last.then_inc(gu_ready, 1)
                        if e:
                            down(e - 1, j, c)
                        elif known(j, 1):
                            down(EXPERTS - 1, j - 1, c)

                def tail(j, t):
                    for c in range(2):
                        down(EXPERTS - 1, j, c)

                run_groups(pe, FRONT_PE, front, expert, tail)


_OUT = ((BATCH, SEQ, DM), "float32")


def kernel(**inputs):
    import numpy as _np
    import concourse.bacc as _bacc
    from concourse import mybir as _mybir
    from concourse.bass_utils import run_bass_kernel_spmd as _run

    nc = _bacc.Bacc("TRN2", target_bir_lowering=False, num_devices=1)
    rel = _np.minimum(_np.arange(1 - SEQ, SEQ + 1, dtype=_np.float32), SEQ - 1)
    rel_log = (_np.sign(rel) * _np.log1p(_np.abs(rel))).astype(_np.float32)
    arrays, args = {}, []

    def give(name, a):
        a = _np.ascontiguousarray(a)
        arrays[name] = a
        args.append(nc.dram_tensor(name, a.shape, _mybir.dt.from_np(a.dtype), kind="ExternalInput").ap())

    for name in ("L0_attn_x", "L0_attn_w_qkv", "L0_attn_b_qkv", "L0_attn_w_out", "L0_attn_b_out",
                 "L0_attn_w1_rpe", "L0_attn_b1_rpe", "L0_attn_w2_rpe", "L0_attn_b2_rpe"):
        give("in_" + name, inputs[name])
    give("in_router", _np.asarray(inputs["L0_ffn_router_w"]).T)
    for name in ("L0_ffn_w_gate", "L0_ffn_w_up", "L0_ffn_w_down"):
        give("in_" + name, inputs[name])
    give("rel_log", rel_log)
    args.append(nc.dram_tensor("out_0", _OUT[0], _mybir.dt.from_np(_np.dtype(_OUT[1])), kind="ExternalOutput").ap())
    build(nc, *args)
    r = _run(nc, [arrays], core_ids=[0])
    return r.results[0]["out_0"]
```

```python
import concourse.bass as bass
from concourse import mybir
from contextlib import ExitStack


FP32 = mybir.dt.float32
BF16 = mybir.dt.bfloat16
U32 = mybir.dt.uint32
ALU = mybir.AluOpType
ACT = mybir.ActivationFunctionType
AX = mybir.AxisListType

BATCH, SEQ, DM = 4, 1024, 128
HEADS, DH = 16, 8
RPE = 32
EXPERTS, HID = 8, 256
P = 128
TILES = BATCH * SEQ // P
CH = SEQ // P
GROUPS = TILES // 4
PLANES = 3
ROWS = 96
SHIFT_ROWS = 2 * CH
KROWS = ROWS + SHIFT_ROWS
PLANE_WORDS = PLANES * TILES * P
TABW = SEQ + SEQ - P
NREL = 2 * SEQ

UNITS = HEADS * BATCH
STEPS = UNITS * CH
LEAD = 12
LAG = 3
NORM_AT, SHIFT_AT, COPY_AT = 4, 6, 7
CHAIN = 14
BIAS_BY = ("PM", "AA", "MM", "MM", "MA", "MM", "MM", "MA")
LAST_BIAS_BY = ("AA", "MM", "AA", "MM", "AA", "MM", "AA", "AA")
PE_HALVES = [(k, h) for k in range(CH) for h in range(2) if BIAS_BY[k][h] == "P"]
PARTS_LOADED = PLANES * len(PE_HALVES) * 16
EARLY_POOL = 506
EARLY_PE, EARLY_DVE, EARLY_ACT = (503, 505, 509), (506, 506, 508), (500, 504, 510)
ADDED = sum(by.count("A") for by in BIAS_BY)
MULTIPLIED = sum("M" in by for by in BIAS_BY)
BODY = 8 * CH
FIRST = 24
TURNS = (STEPS - FIRST - LEAD) // BODY
LOOP_END = FIRST + TURNS * BODY
FRONT_PE = (1, 2, 9, 11)
FRONT_DVE = (4, 6, 8, 12, 14, 15)
FRONT_ACT = (0, 1, 10, 13)


def unit_bias_by(g):
    return LAST_BIAS_BY if g // CH == UNITS - 1 else BIAS_BY


def bias_by(g):
    return unit_bias_by(g)[g % CH]


def added_before(g):
    return sum(by.count("A") for by in unit_bias_by(g)[:g % CH])


def multiplied_before(g):
    return sum("M" in by for by in unit_bias_by(g)[:g % CH])


def exists(kind, g):
    n = g // CH
    if kind == "max":
        return 0 <= g + LEAD < STEPS
    if kind == "exp":
        return 0 <= g < STEPS
    if kind == "pv":
        return 0 <= g - LAG < STEPS
    if kind == "norm":
        return g % CH == NORM_AT and 1 <= n <= UNITS
    return g % CH == SHIFT_AT and 0 <= n + 1 < UNITS


def wait_apart(engine, semaphore, value, passed):
    engine.wait_ge(semaphore, value)
    engine.sem_inc(passed, 1)


def build(nc, x, w_qkv, b_qkv, w_out, b_out, w1, b1, w2, b2, router_w, w_gate, w_up, w_down, rel_log, out):
    q_planes = nc.dram_tensor("q_planes", [BATCH, HEADS, PLANES * DH, SEQ], BF16).ap()
    k_planes = nc.dram_tensor("k_planes", [BATCH, HEADS, (2 * PLANES - 1) * DH, SEQ], BF16).ap()
    bias_rows = nc.dram_tensor("bias_rows", [2, HEADS, NREL], FP32).ap()
    bias_planes = nc.dram_tensor("bias_planes", [PLANES, HEADS, NREL], BF16).ap()

    with ExitStack() as ctx:
        def sb(name, shape, dt=FP32):
            return ctx.enter_context(nc.sbuf_tensor(name, shape, dt))

        xall = sb("xall", [P, TILES, DM])
        vall = sb("vall", [P, TILES, DM])
        oall = sb("oall", [P, TILES, DM])
        wg = sb("wg", [P, EXPERTS, HID])
        wu = sb("wu", [P, EXPERTS, HID])
        wd = sb("wd", [P, EXPERTS, 2, DM])
        wout = sb("wout", [P, DM])
        bout = sb("bout", [P, DM])
        wr = sb("wr", [P, EXPERTS])
        ident = sb("ident", [P, P])
        identb = sb("identb", [P, P], BF16)
        mirror = sb("mirror", [P, P])
        iota8 = sb("iota8", [P, EXPERTS])
        minus_half = sb("minus_half", [P, TILES])
        area = sb("area", [P, PLANE_WORDS + 2 * TABW])
        ps = ctx.enter_context(nc.psum_tensor("ps", [P, 8, 512], FP32))

        qst = [sb(f"qst{i}", [P, SEQ], BF16) for i in range(4)]
        kst = [sb(f"kst{i}", [P, SEQ], BF16) for i in range(4)]
        vst = [sb(f"vst{i}", [P, CH, 32]) for i in range(2)]
        shifts = sb("shifts", [P, CH * SHIFT_ROWS], BF16)

        tabs = [[area[:, at + i * TABW:at + (i + 1) * TABW] for i in range(2)] for at in (PLANE_WORDS, CH * SEQ)]
        tabs_loaded = [[ctx.enter_context(nc.semaphore(f"tab{i}_{n}_loaded")) for n in range(2)] for i in range(2)]
        planes_stored = [ctx.enter_context(nc.semaphore(f"planes_stored{b}")) for b in range(BATCH)]
        qk_loaded = [ctx.enter_context(nc.semaphore(f"qk_loaded{i}")) for i in range(4)]

        def load_tabs(sp, h, turn):
            for n in range(2):
                at = bias_rows[n, h, 0:TABW]
                sp.dma_start(tabs[turn][n], bass.AP(at.tensor, at.offset, [[1, P], [1, TABW]]))\
                  .then_inc(tabs_loaded[turn][n], 16)

        half = PLANE_WORDS // 2
        qp = area[:, 0:half].bitcast(BF16).rearrange("p (j t) -> p j t", j=PLANES)
        kp = area[:, half:2 * half].bitcast(BF16).rearrange("p (j t) -> p j t", j=PLANES)

        def store_planes(sp, b):
            for j in range(PLANES):
                sp.dma_start(q_planes[b, :, j * DH:(j + 1) * DH, :], qp[:, j, b * SEQ:(b + 1) * SEQ])\
                  .then_inc(planes_stored[b], 16)
            for j in range(2 * PLANES - 1):
                sp.dma_start(k_planes[b, :, j * DH:(j + 1) * DH, :], kp[:, j % PLANES, b * SEQ:(b + 1) * SEQ])\
                  .then_inc(planes_stored[b], 16)

        def load_operands(sp, head, b, buf):
            for n in range(PLANES):
                rows = slice(n * PLANES * DH, (n + 1) * PLANES * DH)
                sp.dma_start(qst[buf][rows, :], q_planes[b, head, :, :]).then_inc(qk_loaded[buf], 16)
                sp.dma_start(kst[buf][rows, :], k_planes[b, head, n * DH:(n + PLANES) * DH, :])\
                  .then_inc(qk_loaded[buf], 16)

        front = make_front(nc, ctx, xall, oall, wout, bout, wr, ident, iota8, minus_half, ps)
        prepare(nc, x, w_qkv, b_qkv, w_out, b_out, w1, b1, w2, b2, router_w, w_gate, w_up, w_down, rel_log,
                bias_rows, bias_planes, xall, vall, oall, wg, wu, wd, wout, bout, wr, ident, identb, mirror, iota8,
                minus_half, qp, kp, ps, qst, kst, vst, shifts, planes_stored, store_planes, load_tabs, load_operands)
        attend(nc, bias_planes, vall, oall, ident, identb, area, tabs, tabs_loaded, qk_loaded, ps, qst, kst, vst, shifts,
               planes_stored, store_planes, load_tabs, load_operands, front)
        finish(nc, out, wg, wu, wd, front, ps)


def prepare(nc, x, w_qkv, b_qkv, w_out, b_out, w1, b1, w2, b2, router_w, w_gate, w_up, w_down, rel_log,
            bias_rows, bias_planes, xall, vall, oall, wg, wu, wd, wout, bout, wr, ident, identb, mirror, iota8,
            minus_half, qp, kp, ps, qst, kst, vst, shifts, planes_stored, store_planes, load_tabs, load_operands):
    with ExitStack() as ctx:
        def sb(name, shape, dt=FP32):
            return ctx.enter_context(nc.sbuf_tensor(name, shape, dt))

        def sem(name):
            return ctx.enter_context(nc.semaphore(name))

        wqkv = sb("wqkv", [P, 3 * DM])
        bq = sb("bq", [P, 1])
        bk = sb("bk", [P, 1])
        bv = sb("bv", [P, DM])
        rel = sb("rel", [RPE, NREL])
        hid = sb("hid", [RPE, NREL])
        w1c = sb("w1c", [RPE, 1])
        b1c = sb("b1c", [RPE, 1])
        w2s = sb("w2s", [RPE, HEADS])
        b2c = sb("b2c", [HEADS, 1])
        bias = rel[0:HEADS, :]
        ebias = hid[0:HEADS, :]
        bmax = sb("bmax", [HEADS, 1])
        bias_wide = sb("bias_wide", [P, HEADS * NREL // P])
        bias_rest = sb("bias_rest", [P, HEADS * NREL // P])
        bias_bf = sb("bias_bf", [P, PLANES, HEADS * NREL // P], BF16)
        stats = sb("stats", [P, TILES, 6])
        mv = sb("mv", [P, TILES, 2])
        rstd = sb("rstd", [P, TILES])
        xn = [oall[:, 4 * i:4 * i + 4, :] for i in range(2)]
        kf, qf, qr, *kr = (oall[:, 4 * i:4 * i + 4, :].rearrange("p a d -> p (a d)") for i in range(2, 7))
        xt = [sb(f"xt_q{i}", [P, 512]) for i in range(2)]
        xt_rev = [sb(f"xt_rev{i}", [P, 512]) for i in range(2)]

        x_loaded = [sem(f"x_loaded{b}") for b in range(BATCH)]
        rpe_loaded = sem("rpe_loaded")
        small_loaded = sem("small_loaded")
        weights_loaded = sem("weights_loaded")
        const_ready = sem("const_ready")
        v_zeroed = sem("v_zeroed")
        operands_cleared = sem("operands_cleared")
        stats_ready = sem("stats_ready")
        aggr_ready = sem("aggr_ready")
        rstd_ready = sem("rstd_ready")
        hidden_ready = sem("hidden_ready")
        bias_ps = sem("bias_ps")
        bias_chain = sem("bias_chain")
        bias_ready = sem("bias_ready")
        ebias_ready = sem("ebias_ready")
        bias_wide_loaded = sem("bias_wide_loaded")
        bias_parts_stored = sem("bias_parts_stored")
        bias_part = sem("bias_part")
        bias_rest_ready = sem("bias_rest_ready")
        bias_stored = sem("bias_stored")
        xn_ready = sem("xn_ready")
        xt_ps = sem("xt_ps")
        xt_ready = sem("xt_ready")
        qkv_ps = sem("qkv_ps")
        k_first = sem("k_first")
        k_rest = sem("k_rest")
        k_second = sem("k_second")
        k_split = sem("k_split")
        q_scaled = sem("q_scaled")
        q_first = sem("q_first")
        q_rest = sem("q_rest")
        q_second = sem("q_second")
        q_split = sem("q_split")
        v_ready = sem("v_ready")
        pool_waits = sem("pool_waits1")

        xt_bank, xt_rev_bank = ps[:, 0, :], ps[:, 1, :]
        q_bank, k_bank, v_bank = ([ps[:, 2 + 3 * t + n, :] for t in range(2)] for n in range(3))

        def tokens(j):
            return bass.ds(j * 512, 512)

        def tokens_rev(j, t):
            return bass.ds((j + (1 - 2 * t)) * 512, 512)

        def run_pairs(engine, step):
            for t in range(2):
                step(t, t)
            with engine.Fori(1, BATCH - 1) as b:
                for t in range(2):
                    step(b * 2 + t, t)
            for t in range(2):
                step(GROUPS - 2 + t, t)

        def known(j, least):
            return not isinstance(j, int) or j >= least

        def wide(rows):
            return rows.rearrange("h (a r) -> (h a) r", r=HEADS * NREL // P)

        with nc.Block() as block:
            @block.sync
            def _(sp):
                sp.dma_start(rel[:, :], rel_log.partition_broadcast(RPE)).then_inc(rpe_loaded, 16)
                for dst, src in ((w1c, w1.rearrange("a j -> j a")), (b1c, b1.rearrange("(j a) -> j a", a=1)),
                                 (w2s, w2), (b2c, b2.rearrange("(h a) -> h a", a=1))):
                    sp.dma_start(dst[:, :], src).then_inc(rpe_loaded, 16)
                for dst, src in ((wqkv, w_qkv), (bq, b_qkv[0:DM].rearrange("(c a) -> c a", a=1)),
                                 (bk, b_qkv[DM:2 * DM].rearrange("(c a) -> c a", a=1)),
                                 (bv, b_qkv[2 * DM:3 * DM].partition_broadcast(P))):
                    sp.dma_start(dst[:, :], src).then_inc(small_loaded, 16)
                for dst, src in ((wout[:, :], w_out), (bout[:, :], b_out.partition_broadcast(P)),
                                 (wr[:, :], router_w), (wg[:, :, :], w_gate.rearrange("e d h -> d e h")),
                                 (wu[:, :, :], w_up.rearrange("e d h -> d e h")),
                                 (wd[:, :, :, :], w_down.rearrange("e (c h) d -> h e c d", c=2))):
                    sp.dma_start(dst, src).then_inc(weights_loaded, 16)
                sp.wait_ge(bias_ready, 1)
                sp.dma_start(bias_rows[0, :, :], bias).then_inc(bias_stored, 16)
                sp.wait_ge(ebias_ready, 1)
                sp.dma_start(bias_rows[1, :, :], ebias).then_inc(bias_stored, 16)
                sp.wait_ge(bias_stored, 32)
                sp.dma_start(bias_wide[:, :], wide(bias_rows[0, :, :])).then_inc(bias_wide_loaded, 16)
                load_tabs(sp, 0, 0)

                def store_split(b):
                    sp.wait_ge(q_split, b * 2 + 2)
                    sp.wait_ge(k_split, b * 2 + 2)
                    store_planes(sp, b)

                store_split(0)
                sp.wait_ge(operands_cleared, 4)
                store_split(1)
                sp.wait_ge(planes_stored[0], (3 * PLANES - 1) * 16)
                load_operands(sp, 0, 0, 0)
                sp.wait_ge(planes_stored[1], (3 * PLANES - 1) * 16)
                load_operands(sp, 0, 1, 1)
                sp.wait_ge(bias_rest_ready, 2)
                for n in range(PLANES):
                    sp.dma_start(wide(bias_planes[n, :, :]), bias_bf[:, n, :]).then_inc(bias_parts_stored, 16)
                store_split(2)
                sp.wait_ge(bias_parts_stored, PLANES * 16)
                sp.wait_ge(weights_loaded, 6 * 16)

            @block.gpsimd
            def _(pool):
                pool.memset(ident[:, :], 0.0).then_inc(const_ready, 1)
                pool.memset(identb[:, :], 0.0).then_inc(const_ready, 1)
                pool.memset(minus_half[:, :], -0.5).then_inc(const_ready, 1)
                pool.iota(iota8[:, :], pattern=[[1, EXPERTS]], base=0, channel_multiplier=0,
                          allow_small_or_imprecise_dtypes=True).then_inc(const_ready, 1)
                pool.memset(mirror[:, :], 0.0).then_inc(const_ready, 1)
                pool.wait_ge(const_ready, 5)
                for m in (ident, identb):
                    pool.affine_select(out=m[:, :], in_=m[:, :], compare_op=ALU.not_equal, fill=1.0, base=0,
                                       pattern=[[-1, P]], channel_multiplier=1).then_inc(const_ready, 1)
                pool.affine_select(out=mirror[:, :], in_=mirror[:, :], compare_op=ALU.not_equal, fill=1.0,
                                   base=1 - P, pattern=[[1, P]], channel_multiplier=1).then_inc(const_ready, 1)
                for b in range(BATCH):
                    rows = slice(b * CH, (b + 1) * CH)
                    pool.wait_ge(aggr_ready, b + 1)
                    pool.tensor_scalar(rstd[:, rows], mv[:, rows, 1], 1e-5, None, ALU.add).then_inc(rstd_ready, 1)
                    pool.wait_ge(rstd_ready, 2 * b + 1)
                    pool.tensor_tensor(rstd[:, rows], rstd[:, rows], minus_half[:, rows], ALU.pow)\
                        .then_inc(rstd_ready, 1)

                def last_plane(j, t):
                    wait_apart(pool, k_second, j + 1, pool_waits)
                    pool.tensor_tensor(kp[:, 2, tokens_rev(j, t)], kr[t][:, :], kp[:, 1, tokens_rev(j, t)],
                                       ALU.subtract).then_inc(k_split, 1)

                def step(j, t):
                    if isinstance(j, int) and j == GROUPS - 2:
                        pool.wait_ge(bias_part, 1)
                        pool.tensor_tensor(bias_rest[:, :], bias_wide[:, :], bias_bf[:, 0, :], ALU.subtract)\
                            .then_inc(bias_rest_ready, 1)
                        pool.wait_ge(bias_part, 2)
                        pool.tensor_tensor(bias_bf[:, 2, :], bias_rest[:, :], bias_bf[:, 1, :], ALU.subtract)\
                            .then_inc(bias_rest_ready, 1)
                    if known(j, 1):
                        last_plane(j - 1, 1 - t)
                    if known(j, 2):
                        pool.wait_ge(k_split, j - 1)
                    wait_apart(pool, k_first, j + 1, pool_waits)
                    pool.tensor_tensor(kr[t][:, :], kf[:, :], kp[:, 0, tokens_rev(j, t)], ALU.subtract)\
                        .then_inc(k_rest, 1)


                run_pairs(pool, step)
                last_plane(GROUPS - 1, 1)

            @block.scalar
            def _(act):
                for b in range(BATCH):
                    act.dma_start(xall[:, b * CH:(b + 1) * CH, :], x[b].rearrange("(c p) d -> p c d", p=P))\
                       .then_inc(x_loaded[b], 16)
                act.wait_ge(rpe_loaded, 5 * 16)
                nc.scalar.activation(hid[:, :], rel[:, :], ACT.Relu, bias=b1c[:, :], scale=w1c[:, :])\
                  .then_inc(hidden_ready, 1)

                def second_planes(j, t):
                    act.wait_ge(q_rest, j + 1)
                    nc.scalar.copy(qp[:, 1, tokens(j)], qr[:, :]).then_inc(q_second, 1)
                    act.wait_ge(k_rest, j + 1)
                    nc.scalar.copy(kp[:, 1, tokens_rev(j, t)], kr[t][:, :]).then_inc(k_second, 1)

                def copy_rows(j, t):
                    act.wait_ge(xt_ps, j + 1)
                    nc.scalar.copy(xt[t][:, :], xt_bank)
                    nc.scalar.copy(xt_rev[t][:, :], xt_rev_bank).then_inc(xt_ready, 1)

                def step(j, t):
                    if isinstance(j, int) and j == GROUPS - 2:
                        act.wait_ge(bias_wide_loaded, 16)
                        nc.scalar.copy(bias_bf[:, 0, :], bias_wide[:, :]).then_inc(bias_part, 1)
                        act.wait_ge(bias_rest_ready, 1)
                        nc.scalar.copy(bias_bf[:, 1, :], bias_rest[:, :]).then_inc(bias_part, 1)
                    if not isinstance(j, int) or j + 1 < GROUPS:
                        if known(j, 1):
                            act.wait_ge(qkv_ps, j)
                        copy_rows(j + 1, 1 - t)
                    if isinstance(j, int) and j == 0:
                        act.wait_ge(bias_ready, 1)
                        nc.scalar.activation(ebias, bias, ACT.Exp).then_inc(ebias_ready, 1)
                    if known(j, 1):
                        second_planes(j - 1, 1 - t)
                    act.wait_ge(qkv_ps, j + 1)
                    nc.scalar.activation(kp[:, 0, tokens_rev(j, t)], k_bank[t], ACT.Identity, bias=bk[:, :])
                    nc.scalar.activation(kf[:, :], k_bank[t], ACT.Identity, bias=bk[:, :]).then_inc(k_first, 1)
                    act.wait_ge(q_scaled, j + 1)
                    nc.scalar.copy(qp[:, 0, tokens(j)], qf[:, :]).then_inc(q_first, 1)

                copy_rows(0, 0)
                run_pairs(act, step)
                second_planes(GROUPS - 1, 1)

            @block.vector
            def _(dve):
                def normalise(j, t):
                    for q in range(4):
                        tile = bass.ds(j * 4 + q, 1)
                        last = nc.vector.tensor_scalar(
                            xn[t][:, q, :], xall[:, tile, :].rearrange("p a s -> p (a s)"),
                            mv[:, tile, 0], rstd[:, tile], ALU.subtract, ALU.mult)
                    last.then_inc(xn_ready, 1)

                def clear_operands(i):
                    nc.vector.memset(qst[i][64:ROWS, :], 0.0)
                    nc.vector.memset(kst[i][64:ROWS, :], 0.0)
                    nc.vector.memset(kst[i][ROWS:KROWS, :], 1.0).then_inc(operands_cleared, 1)

                clear_operands(0)
                clear_operands(1)
                for b in range(BATCH):
                    dve.wait_ge(x_loaded[b], 16)
                    for tile in range(b * CH, (b + 1) * CH):
                        last = nc.vector.bn_stats(stats[:, tile, :], xall[:, tile, :])
                    last.then_inc(stats_ready, 1)
                    dve.wait_ge(stats_ready, b + 1)
                    for tile in range(b * CH, (b + 1) * CH):
                        last = nc.vector.bn_aggr(mv[:, tile, :], stats[:, tile, :])
                    last.then_inc(aggr_ready, 1)
                dve.wait_ge(rstd_ready, 2)
                for t in range(2):
                    normalise(t, t)
                clear_operands(2)
                clear_operands(3)
                dve.wait_ge(bias_ps, 1)
                nc.vector.tensor_scalar(bias, ps[0:HEADS, 4:8, :].rearrange("h a b -> h (a b)"), b2c[:, :], None,
                                        ALU.add).then_inc(bias_chain, 1)
                dve.wait_ge(bias_chain, 1)
                nc.vector.reduce_max(bmax[:, :], bias, AX.X).then_inc(bias_chain, 1)
                dve.wait_ge(bias_chain, 2)
                nc.vector.tensor_scalar(bias, bias, bmax[:, :], None, ALU.subtract).then_inc(bias_ready, 1)
                dve.wait_ge(rstd_ready, 2 * BATCH)
                nc.vector.memset(shifts[:, :], 0.0)
                nc.vector.memset(vst[0][:, :, :], 0.0)
                nc.vector.memset(vst[1][:, :, :], 0.0).then_inc(v_zeroed, 1)
                dve.wait_ge(v_zeroed, 1)
                for i in range(2):
                    nc.vector.memset(vst[i][:, :, DH:DH + 1], 1.0)

                def last_plane(j):
                    dve.wait_ge(q_second, j + 1)
                    nc.vector.tensor_tensor(qp[:, 2, tokens(j)], qr[:, :], qp[:, 1, tokens(j)], ALU.subtract)\
                      .then_inc(q_split, 1)

                def step(j, t):
                    if not isinstance(j, int) or j + 2 < GROUPS:
                        dve.wait_ge(xt_ps, j + 1)
                        normalise(j + 2, t)
                    if known(j, 1):
                        last_plane(j - 1)
                    dve.wait_ge(qkv_ps, j + 1)
                    nc.vector.tensor_scalar(qf[:, :], q_bank[t], bq[:, :], float(DH) ** -0.5, ALU.add, ALU.mult)\
                      .then_inc(q_scaled, 1)
                    nc.vector.tensor_tensor(vall[:, bass.ds((j + (1 - 2 * t)) * 4, 4), :],
                                            v_bank[t].rearrange("p (q c) -> p q c", q=4),
                                            bv[:, :].unsqueeze(1).to_broadcast([P, 4, DM]), ALU.add)\
                      .then_inc(v_ready, 1)
                    dve.wait_ge(q_first, j + 1)
                    nc.vector.tensor_tensor(qr[:, :], qf[:, :], qp[:, 0, tokens(j)], ALU.subtract)\
                      .then_inc(q_rest, 1)

                run_pairs(dve, step)
                last_plane(GROUPS - 1)

            @block.tensor
            def _(pe):
                pe.wait_ge(hidden_ready, 1)
                for i in range(4):
                    last = nc.tensor.matmul(ps[0:HEADS, 4 + i, :], w2s[:, :], hid[:, i * 512:(i + 1) * 512],
                                            start=True, stop=True)
                last.then_inc(bias_ps, 1)
                pe.wait_ge(const_ready, 8)

                def transpose(j, t):
                    pe.wait_ge(xn_ready, j + 1)
                    if known(j, 1):
                        pe.wait_ge(xt_ready, j)
                    for q in range(4):
                        nc.tensor.transpose(xt_bank[:, q * P:(q + 1) * P], xn[t][:, q, :], ident[:, :])
                        last = nc.tensor.transpose(xt_rev_bank[:, (3 - q) * P:(4 - q) * P], xn[t][:, q, :],
                                                   mirror[:, :])
                    last.then_inc(xt_ps, 1)

                def step(j, t):
                    if not isinstance(j, int) or j + 1 < GROUPS:
                        transpose(j + 1, 1 - t)
                    pe.wait_ge(xt_ready, j + 1)
                    if known(j, 2):
                        pe.wait_ge(v_ready, j - 1)
                        pe.wait_ge(k_first, j - 1)
                    nc.tensor.matmul(q_bank[t], wqkv[:, 0:DM], xt[t][:, :], start=True, stop=True)
                    nc.tensor.matmul(k_bank[t], wqkv[:, DM:2 * DM], xt_rev[t][:, :], start=True, stop=True)
                    for q in range(4):
                        last = nc.tensor.matmul(v_bank[t][:, q * P:(q + 1) * P], xt_rev[t][:, q * P:(q + 1) * P],
                                                wqkv[:, 2 * DM:3 * DM], start=True, stop=True)
                    last.then_inc(qkv_ps, 1)

                transpose(0, 0)
                pe.wait_ge(small_loaded, 4 * 16)
                pe.wait_ge(bias_chain, 1)
                run_pairs(pe, step)


class Front:
    def __init__(self, act, dve, pe, pool, known, y, xt, ge, xt_ready, chain, stored):
        self.act, self.dve, self.pe, self.pool = act, dve, pe, pool
        self.known, self.y, self.xt, self.ge = known, y, xt, ge
        self.xt_ready, self.chain, self.stored = xt_ready, chain, stored


def make_front(nc, ctx, xall, oall, wout, bout, wr, ident, iota8, minus_half, ps):
    def sb(name, shape, dt=FP32):
        return ctx.enter_context(nc.sbuf_tensor(name, shape, dt))

    def sem(name):
        return ctx.enter_context(nc.semaphore(name))

    o_in = sb("o_in", [P, 4, DM])
    o_t = sb("o_t", [P, 512])
    y = [sb(f"y{i}", [P, 4, DM]) for i in range(2)]
    stats = sb("stats2", [P, 4, 6])
    mv = sb("mv2", [P, 4, 2])
    rstd = sb("rstd2", [P, 4])
    xn = sb("xn2", [P, 4, DM])
    xt = [sb(f"xt{i}", [P, 512]) for i in range(2)]
    logits = sb("logits", [P, 4, EXPERTS])
    top = sb("top", [P, 4, EXPERTS])
    top_at = sb("top_at", [P, 4, EXPERTS], U32)
    at = sb("at", [P, 4, 2])
    sig = sb("sig", [P, 4, 2])
    total = sb("total", [P, 4])
    gates = sb("gates", [P, 4, 2])
    gate1 = sb("gate1", [P, 4, EXPERTS])
    gate2 = sb("gate2", [P, 4, EXPERTS])
    ge = [sb(f"ge{i}", [P, 4, EXPERTS]) for i in range(2)]

    late_ps = [ps[:, 6 + i, :] for i in range(2)]
    early_ps = [ps[:, i, :] for i in range(2)]

    o_staged = sem("o_staged")
    o_t_ps = sem("o_t_ps")
    o_t_ready = sem("o_t_ready")
    proj_ps = sem("proj_ps")
    var_ready = sem("var_ready")
    rstd_ready = sem("rstd_ready2")
    xn_ready = sem("xn_ready2")
    xt_ps = sem("xt_ps2")
    xt_ready = sem("xt_ready2")
    logits_ps = sem("logits_ps")
    top_ready = sem("top_ready")
    sig_ready = sem("sig_ready")
    chain = sem("chain")
    pow_chain = sem("pow_chain")
    dve_waits = sem("dve_waits3")
    pool_waits = sem("pool_waits3")
    stored = [sem(f"stored{i}") for i in range(2)]

    def side(n, j):
        return early_ps if n < 3 and isinstance(j, int) and j == 0 else late_ps

    def known(j, least):
        return not isinstance(j, int) or j >= least

    def front_pool(pool, j):
        wait_apart(pool, var_ready, j + 1, pool_waits)
        pool.tensor_scalar(rstd[:, :], mv[:, :, 1], 1e-5, None, ALU.add).then_inc(pow_chain, 1)
        pool.wait_ge(pow_chain, j + 1)
        pool.tensor_tensor(rstd[:, :], rstd[:, :], minus_half[:, 0:4], ALU.pow).then_inc(rstd_ready, 1)

    def front_act(act, n, j, t):
        if n == 0:
            if known(j, 1):
                act.wait_ge(o_t_ps, j)
            nc.scalar.copy(o_in[:, :, :], oall[:, bass.ds(j * 4, 4), :]).then_inc(o_staged, 1)
        if n == 1:
            act.wait_ge(o_t_ps, j + 1)
            if known(j, 1):
                act.wait_ge(proj_ps, j)
            nc.scalar.copy(o_t[:, :], side(n, j)[0]).then_inc(o_t_ready, 1)
        if n == 2:
            act.wait_ge(xt_ps, j + 1)
            nc.scalar.copy(xt[t][:, :], side(n, j)[0]).then_inc(xt_ready, 1)
        if n == 3:
            act.wait_ge(top_ready, j + 1)
            nc.scalar.activation(sig[:, :, :], top[:, :, 0:2], ACT.Sigmoid).then_inc(sig_ready, 1)

    def stored_before(j, t):
        return j * 8 - 8 * t

    def front_dve(dve, n, j, t):
        base = j * CHAIN
        if n == 0:
            dve.wait_ge(proj_ps, j + 1)
            if known(j, 2):
                if isinstance(j, int):
                    dve.wait_ge(stored[t], j // 2 * 16)
                else:
                    dve.wait_ge(stored[t], stored_before(j, t))
            nc.vector.tensor_tensor(y[t][:, :, :], side(n, j)[1].rearrange("p (q c) -> p q c", q=4),
                                    xall[:, bass.ds(j * 4, 4), :], ALU.add).then_inc(chain, 1)
            dve.wait_ge(chain, base + 1)
            nc.vector.tensor_tensor(y[t][:, :, :], y[t][:, :, :],
                                    bout[:, :].unsqueeze(1).to_broadcast([P, 4, DM]), ALU.add)\
              .then_inc(chain, 1)
        if n == 1:
            dve.wait_ge(chain, base + 2)
            for q in range(4):
                last = nc.vector.bn_stats(stats[:, q, :], y[t][:, q, :])
            last.then_inc(chain, 1)
            wait_apart(dve, chain, base + 3, dve_waits)
            for q in range(4):
                last = nc.vector.bn_aggr(mv[:, q, :], stats[:, q, :])
            last.then_inc(var_ready, 1)
        if n == 2:
            dve.wait_ge(var_ready, j + 1)
            dve.wait_ge(rstd_ready, j + 1)
            for q in range(4):
                last = nc.vector.tensor_scalar(xn[:, q, :], y[t][:, q, :], mv[:, q, 0:1],
                                               rstd[:, q:q + 1], ALU.subtract, ALU.mult)
            last.then_inc(xn_ready, 1)
        if n == 3:
            dve.wait_ge(logits_ps, j + 1)
            nc.vector.tensor_copy(logits[:, :, :], side(n, j)[1][:, 0:4 * EXPERTS]
                                  .rearrange("p (q e) -> p q e", q=4)).then_inc(chain, 1)
            wait_apart(dve, chain, base + 4, dve_waits)
            for q in range(4):
                last = nc.vector.max(top[:, q, :], logits[:, q, :])
            last.then_inc(top_ready, 1)
            wait_apart(dve, top_ready, j + 1, dve_waits)
            for q in range(4):
                last = nc.vector.max_index(top_at[:, q, :], top[:, q, :], logits[:, q, :])
            last.then_inc(chain, 1)
        if n == 4:
            dve.wait_ge(chain, base + 5)
            nc.vector.tensor_copy(at[:, :, :], top_at[:, :, 0:2]).then_inc(chain, 1)
            dve.wait_ge(sig_ready, j + 1)
            nc.vector.tensor_tensor(total[:, :], sig[:, :, 0], sig[:, :, 1], ALU.add).then_inc(chain, 1)
            dve.wait_ge(chain, base + 7)
            nc.vector.tensor_scalar(total[:, :], total[:, :], 1e-10, None, ALU.add).then_inc(chain, 1)
            dve.wait_ge(chain, base + 8)
            nc.vector.reciprocal(total[:, :], total[:, :]).then_inc(chain, 1)
            dve.wait_ge(chain, base + 9)
            nc.vector.tensor_tensor(gates[:, :, :], sig[:, :, :],
                                    total[:, :].unsqueeze(2).to_broadcast([P, 4, 2]), ALU.mult)\
              .then_inc(chain, 1)
        if n == 5:
            dve.wait_ge(chain, base + 10)
            for w, dst in enumerate((gate1, gate2)):
                for q in range(4):
                    last = nc.vector.tensor_scalar(dst[:, q, :], iota8[:, :], at[:, q, w:w + 1],
                                                   gates[:, q, w:w + 1], ALU.is_equal, ALU.mult)
                last.then_inc(chain, 1)
            dve.wait_ge(chain, base + 12)
            nc.vector.tensor_tensor(ge[t][:, :, :], gate1[:, :, :], gate2[:, :, :], ALU.add)\
              .then_inc(chain, 2)

    def front_pe(pe, n, j, t):
        if n == 0:
            pe.wait_ge(o_staged, j + 1)
            if known(j, 1):
                pe.wait_ge(xt_ready, j)
            for q in range(4):
                last = nc.tensor.transpose(side(n, j)[0][:, q * P:(q + 1) * P], o_in[:, q, :], ident[:, :])
            last.then_inc(o_t_ps, 1)
        if n == 1:
            pe.wait_ge(o_t_ready, j + 1)
            if known(j, 1):
                pe.wait_ge(top_ready, j)
            for q in range(4):
                last = nc.tensor.matmul(side(n, j)[1][:, q * P:(q + 1) * P], o_t[:, q * P:(q + 1) * P],
                                        wout[:, :], start=True, stop=True)
            last.then_inc(proj_ps, 1)
        if n == 2:
            pe.wait_ge(xn_ready, j + 1)
            for q in range(4):
                last = nc.tensor.transpose(side(n, j)[0][:, q * P:(q + 1) * P], xn[:, q, :], ident[:, :])
            last.then_inc(xt_ps, 1)
        if n == 3:
            pe.wait_ge(xt_ready, j + 1)
            pe.wait_ge(var_ready, j + 1)
            for q in range(4):
                last = nc.tensor.matmul(side(n, j)[1][:, q * EXPERTS:(q + 1) * EXPERTS],
                                        xt[t][:, q * P:(q + 1) * P], wr[:, :], start=True, stop=True)
            last.then_inc(logits_ps, 1)

    return Front(front_act, front_dve, front_pe, front_pool, known, y, xt, ge, xt_ready, chain, stored)


def attend(nc, bias_planes, vall, oall, ident, identb, area, tabs, tabs_loaded, qk_loaded, ps, qst, kst, vst, shifts,
           planes_stored, store_planes, load_tabs, load_operands, front):
    with ExitStack() as ctx:
        def sb(name, shape, dt=FP32):
            return ctx.enter_context(nc.sbuf_tensor(name, shape, dt))

        def sem(name):
            return ctx.enter_context(nc.semaphore(name))

        prob = [area[:, k * SEQ:(k + 1) * SEQ] for k in range(CH)]
        bias_tab, mul_tab = ([tabs[turn][n] for turn in range(2)] for n in range(2))
        bias_tab_loaded, mul_tab_loaded = ([tabs_loaded[turn][n] for turn in range(2)] for n in range(2))
        bias_parts = [sb(f"bias_parts{i}", [P, PLANES, max(1, len(PE_HALVES)), 512], BF16) for i in range(2)]
        row_max = [sb(f"row_max{i}", [P, CH]) for i in range(2)]
        ot_sb = [sb(f"ot_sb{i}", [P, 256]) for i in range(2)]
        rden = [sb(f"rden{i}", [P, 2, 4]) for i in range(2)]

        max_ps = [ps[:, 2 * i:2 * i + 2, :].rearrange("p a b -> p (a b)") for i in range(2)]
        exp_ps = [ps[:, 4 + h, :] for h in range(2)]
        ot_ps = [ps[:, 6 + i, 0:256] for i in range(2)]
        norm_in = [ps[:, 6 + i, 256:512] for i in range(2)]
        shift_rows = [ps[ROWS:KROWS, 6 + i, :].bitcast(BF16) for i in range(2)]

        parts_loaded = [sem(f"parts_loaded{i}") for i in range(2)]
        max_scores = sem("max_scores")
        exp_scores = sem("exp_scores")
        shift_ps = sem("shift_ps")
        norm_ps = sem("norm_ps")
        pv_done = sem("pv_done")
        max_done = sem("max_done")
        shifts_high = sem("shifts_high")
        shifts_ready = sem("shifts_ready")
        bias_added = sem("bias_added")
        recip_done = sem("recip_done")
        dve_waits = sem("dve_waits2")
        norm_done = sem("norm_done")
        shift_copied = sem("shift_copied")
        v_staged = sem("v_staged")
        exp_done = sem("exp_done")
        ot_copied = sem("ot_copied")
        bias_multiplied = sem("bias_multiplied")

        def count_steps(r, i, more=0):
            return i * BODY + (r + more)

        def count_halves(r, i, more):
            return i * (2 * BODY) + (2 * r + more)

        def count_units(r, i, more=0, per=1):
            return i * (BODY // CH * per) + (r // CH + more) * per

        def run_steps(engine, step):
            for g in range(-LEAD, FIRST):
                step(g, 0, g)
            with engine.Fori(0, TURNS) as i:
                for r in range(FIRST, FIRST + BODY):
                    step(r, i, r)
            for g in range(LOOP_END, STEPS + CH):
                step(g, 0, g)

        with nc.Block() as block:
            @block.sync
            def _(sp):
                def load_parts(h, turn):
                    for n in range(PLANES):
                        for m, (k, half) in enumerate(PE_HALVES):
                            at = bias_planes[n, h, k * P + half * 512:k * P + (half + 1) * 512]
                            sp.dma_start(bias_parts[turn][:, n, m, :],
                                         bass.AP(at.tensor, at.offset, [[1, P], [1, 512]]))\
                              .then_inc(parts_loaded[turn], 16)

                def unit(u, i):
                    h, turn = u // BATCH, u // BATCH % 2
                    if u % BATCH == 0 and u >= 8:
                        sp.wait_ge(pv_done, i * BODY + (h - 1) * BATCH * CH)
                        load_tabs(sp, i * 2 + h, turn)
                        load_parts(i * 2 + h, turn)
                    if u >= 4:
                        sp.wait_ge(exp_scores, i * (2 * BODY) + (u - 3) * (2 * CH))
                    load_operands(sp, i * 2 + h, u % BATCH, u % 4)

                sp.wait_ge(planes_stored[2], (3 * PLANES - 1) * 16)
                unit(2, 0)
                load_parts(0, 0)
                store_planes(sp, BATCH - 1)
                sp.wait_ge(planes_stored[BATCH - 1], (3 * PLANES - 1) * 16)
                unit(BATCH - 1, 0)
                load_tabs(sp, 1, 1)
                load_parts(1, 1)
                for u in range(4, 8):
                    unit(u, 0)
                with sp.Fori(0, UNITS // 8 - 1) as i:
                    for u in range(8, 16):
                        unit(u, i)

            @block.gpsimd
            def _(pool):
                def multiply(r, i, g, k, turn):
                    if r % (BATCH * CH) == min(c for c in range(CH) if "M" in BIAS_BY[c]):
                        pool.wait_ge(mul_tab_loaded[turn], i * 16 + (r // (2 * BATCH * CH) + 1) * 16)
                    pool.wait_ge(exp_done, count_halves(r, i, 2))
                    here = slice(bias_by(g).index("M") * 512, (bias_by(g).rindex("M") + 1) * 512)
                    pool.tensor_tensor(prob[k][:, here], prob[k][:, here], mul_tab[turn][:, k * P:k * P + SEQ][:, here],
                                       ALU.mult).then_inc(bias_multiplied, 1)

                def step(r, i, g):
                    k, turn = r % CH, r // (BATCH * CH) % 2
                    if exists("exp", g) and "M" in bias_by(g):
                        multiply(r, i, g, k, turn)
                    if g == EARLY_POOL:
                        front.pool(pool, 0)

                run_steps(pool, step)

            @block.scalar
            def _(act):
                def step(r, i, g):
                    k, u = r % CH, r // CH
                    if k == COPY_AT and exists("shift", g - k + SHIFT_AT):
                        act.wait_ge(shift_ps, count_units(r, i, 2))
                        nc.scalar.copy(qst[(u + 1) % 4][ROWS:KROWS, :], shift_rows[(u + 1) % 2])\
                          .then_inc(shift_copied, 1)
                    if exists("exp", g) and k == 0:
                        if u >= 2:
                            act.wait_ge(pv_done, count_units(r, i, -1, CH))
                        b, h8 = u % BATCH, i * (2 * DH) + u // BATCH * DH
                        nc.scalar.copy(vst[u % 2][:, :, 0:DH], vall[:, b * CH:(b + 1) * CH, bass.ds(h8, DH)])\
                          .then_inc(v_staged, 1)
                    if exists("exp", g):
                        if r >= CH:
                            act.wait_ge(pv_done, count_steps(r, i, 1 - CH))
                        if g == 0:
                            act.wait_ge(planes_stored[BATCH - 1], (3 * PLANES - 1) * 16)
                        for h in range(2):
                            if bias_by(g)[h] == "A":
                                act.wait_ge(bias_added, count_units(r, i, 0, ADDED)
                                            + (added_before(g) + bias_by(g)[:h + 1].count("A")))
                            else:
                                act.wait_ge(exp_scores, count_halves(r, i, h + 1))
                            nc.scalar.activation(prob[k][:, h * 512:(h + 1) * 512], exp_ps[h], ACT.Exp)\
                              .then_inc(exp_done, 1)
                    if k == LAG and u >= 1 and exists("norm", g - k + NORM_AT):
                        act.wait_ge(pv_done, count_units(r, i, 0, CH))
                        if u >= 3:
                            act.wait_ge(norm_ps, count_units(r, i, -2))
                        nc.scalar.copy(ot_sb[(u - 1) % 2][:, :], ot_ps[(u - 1) % 2]).then_inc(ot_copied, 1)

                    for n in range(3):
                        if g == EARLY_ACT[n]:
                            if n == 0:
                                act.wait_ge(norm_done, UNITS - BATCH + 1)
                            front.act(act, n, 0, 0)

                run_steps(act, step)

            @block.vector
            def _(dve):
                def step(r, i, g):
                    k, u = r % CH, r // CH
                    if exists("exp", g):
                        turn = r // (BATCH * CH) % 2
                        for h in range(2):
                            if bias_by(g)[h] != "A":
                                continue
                            at = k * P + h * 512
                            dve.wait_ge(exp_scores, count_halves(r, i, h + 1))
                            nc.vector.tensor_tensor(exp_ps[h], exp_ps[h], bias_tab[turn][:, at:at + 512], ALU.add)\
                              .then_inc(bias_added, 1)
                    if exists("max", g):
                        a = r + LEAD
                        ka, ua, turn = a % CH, a // CH, a // (BATCH * CH) % 2
                        if a % (BATCH * CH) == 0:
                            dve.wait_ge(bias_tab_loaded[turn], i * 16 + (a // (2 * BATCH * CH) + 1) * 16)
                        if ka == 0 and ua >= 2:
                            dve.wait_ge(shifts_ready, count_units(a, i, -1))
                        wait_apart(dve, max_scores, count_steps(a, i, 1), dve_waits)
                        nc.vector.tensor_tensor_reduce(
                            out=max_ps[k % 2], in0=max_ps[k % 2],
                            in1=bias_tab[turn][:, ka * P:ka * P + SEQ], scale=1.0,
                            scalar=-3.0e38, op0=ALU.add, op1=ALU.max,
                            accum_out=row_max[ua % 2][:, ka:ka + 1]).then_inc(max_done, 1)
                    if exists("max", g) and ka == CH - 1:
                        dve.wait_ge(max_done, count_steps(a, i, 1))
                        if ua >= 1:
                            dve.wait_ge(shift_ps, count_units(a, i))
                        nc.vector.tensor_scalar(shifts[:, 0:CH * SHIFT_ROWS:SHIFT_ROWS + 1], row_max[ua % 2][:, :],
                                                -1.0, None, ALU.mult).then_inc(shifts_high, 1)
                        dve.wait_ge(shifts_high, count_units(a, i, 1))
                        nc.vector.scalar_tensor_tensor(shifts[:, CH:CH * SHIFT_ROWS:SHIFT_ROWS + 1],
                                                       row_max[ua % 2][:, :], -1.0,
                                                       shifts[:, 0:CH * SHIFT_ROWS:SHIFT_ROWS + 1],
                                                       ALU.mult, ALU.subtract).then_inc(shifts_ready, 1)
                    if exists("norm", g):
                        dve.wait_ge(norm_ps, count_units(r, i))
                        o = norm_in[(u - 1) % 2].rearrange("p (i j c) -> p i j c", i=2, j=4)
                        nc.vector.reciprocal(rden[u % 2][:, :, :], o[:, :, :, DH]).then_inc(recip_done, 1)
                        dve.wait_ge(recip_done, count_units(r, i))
                        b, h8 = (u - 1) % BATCH, i * (2 * DH) + (u - 1) // BATCH * DH
                        dst = oall[:, b * CH:(b + 1) * CH, bass.ds(h8, DH)].rearrange("p (j i) d -> p i j d", j=4)
                        nc.vector.tensor_tensor(dst, o[:, :, :, 0:DH],
                                                rden[u % 2][:, :, :].unsqueeze(3).to_broadcast([P, 2, 4, DH]), ALU.mult)\
                          .then_inc(norm_done, 1)

                    for n in range(3):
                        if g == EARLY_DVE[n]:
                            front.dve(dve, n, 0, 0)

                run_steps(dve, step)
                dve.wait_ge(norm_done, UNITS)

            @block.tensor
            def _(pe):
                def step(r, i, g):
                    k, u = r % CH, r // CH
                    if exists("max", g):
                        a = r + LEAD
                        ka, ua = a % CH, a // CH
                        if ka == 0:
                            pe.wait_ge(qk_loaded[ua % 4], i * (2 * 96) + (ua // 4 + 1) * 96)
                        if g + LEAD >= 2:
                            pe.wait_ge(max_done, count_steps(a, i, -1))
                        q, kk, dst = qst[ua % 4], kst[ua % 4], max_ps[k % 2]
                        for c in range(2):
                            last = nc.tensor.matmul(dst[:, c * 512:(c + 1) * 512], q[0:ROWS, ka * P:(ka + 1) * P],
                                                    kk[0:ROWS, c * 512:(c + 1) * 512], start=True, stop=True)
                        last.then_inc(max_scores, 1)
                    if exists("exp", g):
                        if k == 0:
                            pe.wait_ge(shift_copied, count_units(r, i, 1))
                        for h in range(2):
                            if g >= 1:
                                pe.wait_ge(exp_done, count_halves(r, i, h - 1))
                            last = nc.tensor.matmul(exp_ps[h], kst[u % 4][0:KROWS, k * P:(k + 1) * P],
                                                    qst[u % 4][0:KROWS, h * 512:(h + 1) * 512], start=True,
                                                    stop=bias_by(g)[h] != "P")
                            if bias_by(g)[h] == "P":
                                turn = r // (BATCH * CH) % 2
                                if r % (BATCH * CH) == PE_HALVES[0][0] and h == PE_HALVES[0][1]:
                                    pe.wait_ge(parts_loaded[turn], i * PARTS_LOADED
                                               + (r // (2 * BATCH * CH) + 1) * PARTS_LOADED)
                                for n in range(PLANES):
                                    last = nc.tensor.matmul(exp_ps[h], identb[:, :],
                                                            bias_parts[turn][:, n, PE_HALVES.index((k, h)), :],
                                                            start=False, stop=n == PLANES - 1)
                            last.then_inc(exp_scores, 1)
                    if exists("pv", g):
                        c = r - LAG
                        kc, uc = c % CH, c // CH
                        if kc == 0:
                            pe.wait_ge(v_staged, count_units(c, i, 1))
                        if "M" not in bias_by(g - LAG):
                            pe.wait_ge(exp_done, count_halves(c, i, 2))
                        else:
                            pe.wait_ge(bias_multiplied, count_units(c, i, 0, MULTIPLIED)
                                       + (multiplied_before(g - LAG) + 1))
                        for j in range(4):
                            last = nc.tensor.matmul(ot_ps[uc % 2][32 * j:32 * j + 32, :], vst[uc % 2][:, kc, :],
                                                    prob[kc][:, 256 * j:256 * j + 256],
                                                    start=(kc == 0), stop=(kc == CH - 1))
                        last.then_inc(pv_done, 1)
                    if exists("norm", g):
                        pe.wait_ge(ot_copied, count_units(r, i))
                        for c in range(2):
                            last = nc.tensor.transpose(norm_in[(u - 1) % 2][:, c * P:(c + 1) * P],
                                                       ot_sb[(u - 1) % 2][:, c * P:(c + 1) * P], ident[:, :])
                        last.then_inc(norm_ps, 1)
                    if exists("shift", g):
                        if g >= CH:
                            pe.wait_ge(norm_done, count_units(r, i))
                        pe.wait_ge(shifts_ready, count_units(r, i, 2))
                        for c in range(CH):
                            last = nc.tensor.transpose(shift_rows[(u + 1) % 2][:, c * P:(c + 1) * P],
                                                       shifts[:, c * SHIFT_ROWS:(c + 1) * SHIFT_ROWS], identb[:, :])
                        last.then_inc(shift_ps, 1)

                    for n in range(3):
                        if g == EARLY_PE[n]:
                            if n == 0:
                                pe.wait_ge(max_done, STEPS)
                            front.pe(pe, n, 0, 0)

                run_steps(pe, step)


def finish(nc, out, wg, wu, wd, front, ps):
    out_t = out.rearrange("b (c p) d -> p (b c) d", p=P)
    with ExitStack() as ctx:
        def sb(name, shape, dt=FP32):
            return ctx.enter_context(nc.sbuf_tensor(name, shape, dt))

        def sem(name):
            return ctx.enter_context(nc.semaphore(name))

        y, xt, ge, xt_ready, chain, stored, known = (front.y, front.xt, front.ge, front.xt_ready, front.chain,
                                                     front.stored, front.known)
        sg = [sb(f"sg{i}", [P, 512]) for i in range(2)]
        silu = [sb(f"silu{i}", [P, 512]) for i in range(2)]
        hidden = [sb(f"hidden{i}", [P, 2, 512]) for i in range(2)]

        gu_ps = [(ps[:, 2 * c, :], ps[:, 2 * c + 1, :]) for c in range(2)]
        down_ps = [ps[:, 4 + i, :] for i in range(2)]


        gu_ready = sem("gu_ready")
        sg_ready = sem("sg_ready")
        silu_ready = sem("silu_ready")
        hidden_ready = sem("hidden_ready2")
        down_ready = sem("down_ready")
        added = sem("added")


        def run_groups(engine, parts_at, front, first_parts, expert, tail):
            def group(j, after, t):
                for e in range(EXPERTS):
                    for c in range(2):
                        expert(e, c, j, t)
                        for n, at in enumerate(parts_at):
                            if at == 2 * e + c and after is not None:
                                front(n, after, 1 - t)

            for n in first_parts:
                front(n, 0, 0)
            group(0, 1, 0)
            with engine.Fori(0, GROUPS // 2 - 1) as i:
                for t in (1, 0):
                    group(i * 2 + (2 - t), i * 2 + (3 - t), t)
            group(GROUPS - 1, None, 1)
            tail(GROUPS - 1, 1)

        with nc.Block() as block:
            @block.sync
            def _(sp):
                def store(j, t):
                    sp.wait_ge(added, j * EXPERTS + EXPERTS)
                    sp.dma_start(out_t[:, bass.ds(j * 4, 4), :], y[t][:, :, :]).then_inc(stored[t], 16)

                with sp.Fori(0, GROUPS // 2) as i:
                    for t in range(2):
                        store(i * 2 + t, t)
                for t in range(2):
                    sp.wait_ge(stored[t], GROUPS // 2 * 16)

            @block.gpsimd
            def _(pool):
                with pool.Fori(1, GROUPS) as j:
                    front.pool(pool, j)

            @block.scalar
            def _(act):
                def expert(e, c, j, t):
                    m = 2 * e + c
                    act.wait_ge(gu_ready, j * 16 + (m + 1))
                    if m >= 2 or known(j, 1):
                        act.wait_ge(silu_ready, j * 16 + (m - 1))
                    nc.scalar.activation(sg[c][:, :], gu_ps[c][0], ACT.Sigmoid).then_inc(sg_ready, 1)

                run_groups(act, FRONT_ACT, lambda n, j, t: front.act(act, n, j, t), (3,), expert, lambda j, t: None)

            @block.vector
            def _(dve):
                def add_expert(e, j, t):
                    dve.wait_ge(down_ready, j * EXPERTS + (e + 1))
                    if e:
                        dve.wait_ge(added, j * EXPERTS + e)
                    else:
                        dve.wait_ge(chain, j * CHAIN + CHAIN)
                    for q in range(4):
                        last = nc.vector.scalar_tensor_tensor(
                            y[t][:, q, :], down_ps[e % 2][:, q * P:(q + 1) * P], ge[t][:, q, e:e + 1],
                            y[t][:, q, :], ALU.mult, ALU.add)
                    last.then_inc(added, 1)

                def expert(e, c, j, t):
                    m = 2 * e + c
                    dve.wait_ge(sg_ready, j * 16 + (m + 1))
                    if m >= 2 or known(j, 1):
                        dve.wait_ge(hidden_ready, j * 16 + (m - 1))
                    nc.vector.tensor_tensor(silu[c][:, :], gu_ps[c][0], sg[c][:, :], ALU.mult)\
                      .then_inc(silu_ready, 1)
                    if c == 0 and (e >= 2 or known(j, 1)):
                        dve.wait_ge(down_ready, j * EXPERTS + (e - 1))
                    dve.wait_ge(silu_ready, j * 16 + (m + 1))
                    nc.vector.tensor_tensor(hidden[e % 2][:, c, :], gu_ps[c][1], silu[c][:, :], ALU.mult)\
                      .then_inc(hidden_ready, 1)
                    if c == 1 and e:
                        add_expert(e - 1, j, t)
                    elif c == 1 and known(j, 1):
                        add_expert(EXPERTS - 1, j - 1, 1 - t)

                run_groups(dve, FRONT_DVE, lambda n, j, t: front.dve(dve, n, j, t), (3, 4, 5), expert, lambda j, t: add_expert(EXPERTS - 1, j, t))

            @block.tensor
            def _(pe):
                def down(e, j, part):
                    if part == 0:
                        pe.wait_ge(hidden_ready, j * 16 + (2 * e + 2))
                        if e >= 2 or known(j, 1):
                            pe.wait_ge(added, j * EXPERTS + (e - 1))
                    for q in range(2 * part, 2 * part + 2):
                        for c in range(2):
                            last = nc.tensor.matmul(down_ps[e % 2][:, q * P:(q + 1) * P],
                                                    hidden[e % 2][:, c, q * P:(q + 1) * P], wd[:, e, c, :],
                                                    start=(c == 0), stop=(c == 1))
                    if part == 1:
                        last.then_inc(down_ready, 1)

                def expert(e, c, j, t):
                    if e == 0 and c == 0:
                        pe.wait_ge(xt_ready, j + 1)
                    if e or known(j, 1):
                        pe.wait_ge(hidden_ready, j * 16 + (2 * e + c - 1))
                    for w, dst in ((wg, gu_ps[c][0]), (wu, gu_ps[c][1])):
                        last = nc.tensor.matmul(dst, w[:, e, c * P:(c + 1) * P], xt[t][:, :], start=True, stop=True)
                    last.then_inc(gu_ready, 1)
                    if e:
                        down(e - 1, j, c)
                    elif known(j, 1):
                        down(EXPERTS - 1, j - 1, c)

                def tail(j, t):
                    for c in range(2):
                        down(EXPERTS - 1, j, c)

                run_groups(pe, FRONT_PE, lambda n, j, t: front.pe(pe, n, j, t), (3,), expert, tail)


_OUT = ((BATCH, SEQ, DM), "float32")


def kernel(**inputs):
    import numpy as _np
    import concourse.bacc as _bacc
    from concourse import mybir as _mybir
    from concourse.bass_utils import run_bass_kernel_spmd as _run

    nc = _bacc.Bacc("TRN2", target_bir_lowering=False, num_devices=1)
    rel = _np.minimum(_np.arange(1 - SEQ, SEQ + 1, dtype=_np.float32), SEQ - 1)
    rel_log = (_np.sign(rel) * _np.log1p(_np.abs(rel))).astype(_np.float32)
    arrays, args = {}, []

    def give(name, a):
        a = _np.ascontiguousarray(a)
        arrays[name] = a
        args.append(nc.dram_tensor(name, a.shape, _mybir.dt.from_np(a.dtype), kind="ExternalInput").ap())

    for name in ("L0_attn_x", "L0_attn_w_qkv", "L0_attn_b_qkv", "L0_attn_w_out", "L0_attn_b_out",
                 "L0_attn_w1_rpe", "L0_attn_b1_rpe", "L0_attn_w2_rpe", "L0_attn_b2_rpe"):
        give("in_" + name, inputs[name])
    give("in_router", _np.asarray(inputs["L0_ffn_router_w"]).T)
    for name in ("L0_ffn_w_gate", "L0_ffn_w_up", "L0_ffn_w_down"):
        give("in_" + name, inputs[name])
    give("rel_log", rel_log)
    args.append(nc.dram_tensor("out_0", _OUT[0], _mybir.dt.from_np(_np.dtype(_OUT[1])), kind="ExternalOutput").ap())
    build(nc, *args)
    r = _run(nc, [arrays], core_ids=[0])
    return r.results[0]["out_0"]
```
